# Optimizing a Trainium2 kernel written in Bass

```python
import numpy as np
import jax
import jax.numpy as jnp

def _softmax(x, axis=-1):
    return jax.nn.softmax(x, axis=axis)

def _gelu(x):
    return jax.nn.gelu(x, approximate=True)

def _silu(x):
    return jax.nn.silu(x)

def _sigmoid(x):
    return jax.nn.sigmoid(x)

def _layernorm(x, axis=-1, eps=1e-05):
    m = jnp.mean(x, axis=axis, keepdims=True)
    v = jnp.var(x, axis=axis, keepdims=True)
    return (x - m) / jnp.sqrt(v + eps)

def _scatter_add(tgt, idx, src, axis=0):
    return tgt.at[idx].add(src)

def _segment_sum(src, seg, n):
    return jax.ops.segment_sum(src, seg, n)
kernel_name = 'mk_gnn_preln_d1_gnn_r32_b66e9b'

def setup_inputs(seed: int=0):
    np.random.seed(seed)
    _w = jnp.asarray

    def _rec_inputs():
        import jax
        import jax.numpy as jnp
        _gk = jax.random.key(seed)
        x = -0.000364 + 1 * jax.random.normal(jax.random.fold_in(_gk, 1), (50000, 768), jnp.float32)
        src = jax.random.randint(jax.random.fold_in(_gk, 2), (25000,), 0, 50000, jnp.int32)
        dst = jax.random.randint(jax.random.fold_in(_gk, 3), (25000,), 0, 50000, jnp.int32)
        _o = jnp.argsort(dst, stable=True)
        src = src[_o]
        dst = dst[_o]
        return (x, src, dst)
    x, src, dst = _rec_inputs()

    def _L0_gnn_setup():
        import jax, jax.numpy as jnp
        import numpy as np
        N = 625
        DEG = 16
        E = N * DEG
        H = 12
        DIN = 64
        DOUT = 64
        NEG_SLOPE = 0.2
        key = jax.random.key(seed)
        k_h, k_src, k_w, k_al, k_ar, k_wr = jax.random.split(key, 6)
        std = 1.414 * np.sqrt(2.0 / (DIN + DOUT))
        h = jax.random.normal(k_h, (N, H * DIN), dtype=jnp.float32)
        src = jax.random.randint(k_src, (E,), 0, N, dtype=jnp.int64)
        dst = jnp.repeat(jnp.arange(N, dtype=jnp.int64), DEG)
        W = jax.random.normal(k_w, (DOUT, DIN), dtype=jnp.float32) * std
        attn_l = jax.random.normal(k_al, (1, H, DOUT), dtype=jnp.float32) * std
        attn_r = jax.random.normal(k_ar, (1, H, DOUT), dtype=jnp.float32) * std
        W_res = jax.random.normal(k_wr, (DOUT, DIN), dtype=jnp.float32) * std
        return {'h': h, 'src': src, 'dst': dst, 'W': W, 'attn_l': attn_l, 'attn_r': attn_r, 'W_res': W_res}
    _L0_gnn_all = _L0_gnn_setup()
    _L0_gnn_in = {k: v for k, v in _L0_gnn_all.items() if k in ('W', 'attn_l', 'attn_r', 'W_res')}
    del _L0_gnn_all
    return {'x': x, 'src': src, 'dst': dst, 'L0_gnn_W': _L0_gnn_in['W'], 'L0_gnn_attn_l': _L0_gnn_in['attn_l'], 'L0_gnn_attn_r': _L0_gnn_in['attn_r'], 'L0_gnn_W_res': _L0_gnn_in['W_res']}

def reference(x, src, dst, L0_gnn_W, L0_gnn_attn_l, L0_gnn_attn_r, L0_gnn_W_res):
    import jax
    import jax.numpy as jnp

    def _L0_gnn_ref(h, src, dst, W, attn_l, attn_r, W_res):
        import jax, jax.numpy as jnp
        import numpy as np
        N = 625
        DEG = 16
        E = N * DEG
        H = 12
        DIN = 64
        DOUT = 64
        NEG_SLOPE = 0.2
        n = h.shape[0]
        hv = h.reshape(n, H, DIN)
        ft = jnp.einsum('nhd,od->nho', hv, W)
        a1 = jnp.sum(ft * attn_l, axis=-1)
        a2 = jnp.sum(ft * attn_r, axis=-1)
        e = jax.nn.leaky_relu(a1[src] + a2[dst], negative_slope=NEG_SLOPE)
        m = jax.ops.segment_max(e, dst, num_segments=n)
        m = jnp.where(jnp.isfinite(m), m, 0.0)
        w = jnp.exp(e - m[dst])
        denom = jax.ops.segment_sum(w, dst, num_segments=n)
        alpha = w / jnp.maximum(denom[dst], 1e-16)
        msg = alpha[:, :, None] * ft[src]
        agg = jax.ops.segment_sum(msg, dst, num_segments=n)
        res = jnp.einsum('nhd,od->nho', hv, W_res)
        out = jax.nn.relu((agg + res).reshape(n, H * DOUT))
        return out
    h = jnp.maximum(_layernorm(x, axis=-1), 0.0)
    x = x + _L0_gnn_ref(h, src, dst, L0_gnn_W, L0_gnn_attn_l, L0_gnn_attn_r, L0_gnn_W_res)
    return x

_drawn_inputs = setup_inputs


def setup_inputs(seed=0):
    import zlib

    import numpy as np

    out = dict(_drawn_inputs(seed))
    spreads = {}
    factors = {}
    for name, (base, spread) in spreads.items():
        noise = np.random.default_rng([zlib.crc32(name.encode()), seed]).standard_normal(out[name].shape)
        drawn = base * np.exp(spread * noise) if base else spread * noise
        out[name] = jnp.asarray(drawn.astype(out[name].dtype))
    for name, factor in factors.items():
        out[name] = (out[name] * factor).astype(out[name].dtype)
    return out
```

```python
import concourse.bass as bass
from concourse import mybir
from concourse.alu_op_type import AluOpType as ALU
from contextlib import ExitStack

FP32 = mybir.dt.float32
I32 = mybir.dt.int32
ACT = mybir.ActivationFunctionType
AX = mybir.AxisListType

N, F, E, H, D = 50000, 768, 25000, 12, 64
P = 128
PAIRS = F // P
HALF = F // 2
QUAD = 4
BODY = 8
NT = -(-N // (P * BODY)) * BODY
ITERS = NT // BODY
SHIFTED = QUAD
SHIFT = NT * P - N
FIRST_SHIFTED = NT - SHIFTED
TG, TR = 4, NT // 4
ROWS, ROW = 125, E // 125
WIN = P + 1
PAD = 512
FAR = 1 << 20
LOW = -1.0e30
EPS = 1.0e-5
SLOPE = 0.2
DENOM_MIN = 1.0e-16
AGG_LAG = 5
OUT_LAG = 6
LEAD = 2


class Tile:

    def __init__(self, i, off):
        self.i, self.off = i, off

    def ring(self, n):
        return self.off % n

    def count(self, back=0):
        return self.i * BODY + (self.off + 1 - back)

    def turns(self, n, back=0):
        return self.i * (BODY // n) + (self.off // n + 1 - back)

    def quads(self, back=0):
        return self.i * 2 + (self.off // QUAD + 1 - back)

    def exists(self):
        return not isinstance(self.i, int) or 0 <= self.i * BODY + self.off < NT

    def base(self):
        if isinstance(self.i, int):
            t = self.i * BODY + self.off
            return t * P - (SHIFT if t >= FIRST_SHIFTED else 0)
        return self.i * (BODY * P) + self.off * P


def wait(engine, sem, value):
    if not isinstance(value, int) or value > 0:
        engine.wait_ge(sem, value)


def gnn(nc, x, src, dst, w_t, w, w_res_t, attn_l_t, attn_r_t, out):
    ctx = ExitStack()
    with ctx:
        def sb(name, shape, dt=FP32):
            return ctx.enter_context(nc.sbuf_tensor(name, shape, dt))

        def ps(name, shape):
            return ctx.enter_context(nc.psum_tensor(name, shape, FP32))

        def sem(name):
            return ctx.enter_context(nc.semaphore(name))

        dst_pad = nc.dram_tensor("dst_pad", (1, E + PAD), I32, kind="Internal").ap()
        src_pad = nc.dram_tensor("src_pad", (1, E + PAD), I32, kind="Internal").ap()
        seg_dram = nc.dram_tensor("seg_dram", (NT, 2 * WIN), FP32, kind="Internal").ap()
        v1_dram = nc.dram_tensor("v1_dram", (H, D), FP32, kind="Internal").ap()

        ident = sb("ident", [P, P])
        iota_i = sb("iota_i", [P, P], I32)
        iota_row = sb("iota_row", [P, P])
        neg_half = sb("neg_half", [P, 2])
        w_bd = sb("w_bd", [P, P])
        wres_bd = sb("wres_bd", [P, P])
        w_twice = sb("w_twice", [D, 2, D])
        al_t = sb("al_t", [D, H])
        ar_t = sb("ar_t", [D, H])
        v1_row = sb("v1_row", [H, D])
        v1 = sb("v1", [P, H * D])
        v2 = sb("v2", [P, PAIRS, 32])
        loc_c = sb("loc_c", [P, NT + BODY])
        idx_c = sb("idx_c", [P, NT + BODY], I32)
        base_i = sb("base_i", [TR, TG], I32)
        base_c = sb("base_c", [TR, TG])
        shift_c = sb("shift_c", [TR, TG])
        brow_i = sb("brow_i", [ROWS, NT], I32)
        brow = sb("brow", [ROWS, NT])
        brow_s = sb("brow_s", [ROWS, NT])
        rows_i = sb("rows_i", [ROWS, ROW], I32)
        row_first = sb("row_first", [ROWS, 1])
        before = sb("before", [ROWS, NT])
        ones = sb("ones", [ROWS, 1])
        row_c = sb("row_c", [TR, TG])
        row_i = sb("row_i", [TR, TG], I32)
        row_dst_i = sb("row_dst_i", [TR, TG, ROW], I32)
        row_dst = sb("row_dst", [TR, TG, ROW])
        below = sb("below", [TR, TG, ROW])
        below_n = sb("below_n", [TR, TG])
        start_c = sb("start_c", [TR, TG])
        start_i = sb("start_i", [TR, TG], I32)
        win_dst_i = sb("win_dst_i", [TR, TG, WIN], I32)
        win_src_i = sb("win_src_i", [TR, TG, P], I32)
        win_loc = sb("win_loc", [TR, TG, WIN])
        win_far = sb("win_far", [TR, TG, P])
        win_src = sb("win_src", [TR, TG, P])
        seg = sb("seg", [TR, TG, 2, WIN])
        pad_end = sb("pad_end", [1, 2, PAD], I32)
        x_in = sb("x_in", [P, 8, F])
        g_in = sb("g_in", [P, 4, F])
        stats = sb("stats", [P, 2, 4, 6])
        mv = sb("mv", [P, 2, 2, 2])
        veps = sb("veps", [P, 2, 2])
        rstd = sb("rstd", [P, 2, 2])
        shift = sb("shift", [P, 2, 2])
        hn = sb("hn", [P, 2, F])
        he = sb("he", [P, 8, F])
        prod = sb("prod", [P, 2, F])
        hT = sb("hT", [P, 8, F + P])
        gT = sb("gT", [P, 2, F])
        onehot = sb("onehot", [P, 8, P])
        o = sb("o", [P, 4, F])
        loc = sb("loc", [P, 8])
        idx = sb("idx", [P, 8], I32)
        a1 = sb("a1", [P, 2, QUAD, 32])
        a2T = sb("a2T", [P, P])
        a2 = sb("a2", [P, P])
        segq = sb("segq", [P, 2, 2, WIN])
        z = sb("z", [P, P])
        score = sb("score", [P, P])
        m1 = sb("m1", [P, P])
        m2 = sb("m2", [P, P])
        wt = sb("wt", [P, P])
        s1 = sb("s1", [P, P])
        s2 = sb("s2", [P, P])
        alphaT = sb("alphaT", [P, P])
        alpha = sb("alpha", [P, 2, QUAD, 32])
        tp = ps("tp", [P, 2, 512])
        gp = ps("gp", [P, 2, 512])
        op = ps("op", [P, 2, 512])
        a2T_bank = ps("a2T_bank", [P, 512])
        soft_bank = ps("soft_bank", [P, 512])
        a2T_ps = a2T_bank[:, 0:P]
        a2_ps, z_ps, alpha_ps = (soft_bank[:, P * n:P * n + P] for n in range(3))

        ld_edges = sem("ld_edges")
        ld_w = sem("ld_w")
        ld_v1 = sem("ld_v1")
        padded = sem("padded")
        rows_in = sem("rows_in")
        wins_in = sem("wins_in")
        seg_out = sem("seg_out")
        pool_c = sem("pool_c")
        dve_c = sem("dve_c")
        pe_c = sem("pe_c")
        x_ld = [sem(f"x_ld{n}") for n in range(8)]
        g_ld = [sem(f"g_ld{n}") for n in range(4)]
        o_st = [sem(f"o_st{n}") for n in range(4)]
        seg_ld = [sem(f"seg_ld{n}") for n in range(2)]
        idx_cp = sem("idx_cp")
        loc_cp = sem("loc_cp")
        bn_done = sem("bn_done")
        mv_done = sem("mv_done")
        veps_done = sem("veps_done")
        rstd_done = sem("rstd_done")
        shift_done = sem("shift_done")
        hn_done = sem("hn_done")
        he_done = sem("he_done")
        prod_done = sem("prod_done")
        a1_done = sem("a1_done")
        oh_done = sem("oh_done")
        t_done = sem("t_done")
        hT_done = sem("hT_done")
        a2T_mm = sem("a2T_mm")
        scaled = sem("scaled")
        g_mm = sem("g_mm")
        gT_done = sem("gT_done")
        out_mm = sem("out_mm")
        o_done = sem("o_done")
        a2T_sb = sem("a2T_sb")
        a2_tr = sem("a2_tr")
        a2_sb = sem("a2_sb")
        z_mm = sem("z_mm")
        z_sb = sem("z_sb")
        soft = sem("soft")
        exp_done = sem("exp_done")
        alpha_tr = sem("alpha_tr")
        alpha_sb = sem("alpha_sb")
        SOFT = 9

        block = ctx.enter_context(nc.Block())
        edge_rows = dst.rearrange("(a b) -> a b", b=ROW)
        ready = (dve_c, 15)

        @block.sync
        def _(sp):
            sp.dma_start(rows_i[:, :], edge_rows).then_inc(ld_edges, 16)
            sp.dma_start(dst_pad[:, 0:E], dst.rearrange("(o e) -> o e", o=1)).then_inc(padded, 16)
            sp.dma_start(src_pad[:, 0:E], src.rearrange("(o e) -> o e", o=1)).then_inc(padded, 16)
            sp.wait_ge(pool_c, 2)
            sp.dma_start(dst_pad[:, E:E + PAD], pad_end[:, 0, :]).then_inc(padded, 16)
            sp.dma_start(src_pad[:, E:E + PAD], pad_end[:, 1, :]).then_inc(padded, 16)
            sp.dma_start(w_twice[:, 0, :], w).then_inc(ld_w, 16)
            sp.dma_start(w_twice[:, 1, :], w).then_inc(ld_w, 16)
            sp.dma_start(al_t[:, :], attn_l_t).then_inc(ld_w, 16)
            sp.dma_start(ar_t[:, :], attn_r_t).then_inc(ld_w, 16)
            sp.wait_ge(dve_c, 1)
            for a in range(2):
                sp.dma_start(w_bd[D * a:D * a + D, D * a:D * a + D], w_t).then_inc(ld_w, 16)
                sp.dma_start(wres_bd[D * a:D * a + D, D * a:D * a + D], w_res_t).then_inc(ld_w, 16)

            def load(t):
                wait(sp, o_done, t.count(back=8) * 2)
                sp.dma_start(x_in[:, t.ring(8), :], x[bass.ds(t.base(), P), :]).then_inc(x_ld[t.ring(8)], 16)

            def load_flags(t):
                par = t.off // QUAD % 2
                wait(sp, soft, (t.quads(back=2)) * SOFT)
                first = t.i * BODY + t.off
                flags = seg_dram[bass.ds(first, QUAD), :]
                sp.dma_start(segq[:, par, :, :].rearrange("p a b -> p (a b)"),
                             flags.unsqueeze(1).broadcast_to([QUAD, 32, 2 * WIN])).then_inc(seg_ld[par], 16)

            def store(t):
                if isinstance(t.i, int) and t.i * BODY + t.off == FIRST_SHIFTED:
                    for n in range(4):
                        sp.wait_ge(o_st[n], t.turns(4, back=1) * 16)
                sp.wait_ge(o_done, t.count() * 2)
                sp.dma_start(out[bass.ds(t.base(), P), :], o[:, t.ring(4), :]).then_inc(o_st[t.ring(4)], 16)

            for k in range(LEAD):
                load(Tile(0, k))
            sp.wait_ge(dve_c, 8)
            sp.dma_start(v1_dram, v1_row[:, :]).then_inc(ld_v1, 16)
            sp.wait_ge(ld_v1, 16)
            sp.dma_start(v1[:, :], v1_dram.rearrange("(o h) d -> o (h d)", o=1).broadcast_to([P, H * D])).then_inc(ld_v1, 16)
            sp.wait_ge(*ready)
            sp.dma_start(seg_dram.rearrange("(g r) f -> r g f", g=TG),
                         seg[:, :, :, :].rearrange("r g a b -> r g (a b)")).then_inc(seg_out, 16)
            sp.wait_ge(seg_out, 16)

            def slots(i, ks):
                for k in ks:
                    if k % QUAD == 1 and Tile(i, k - 1).exists():
                        load_flags(Tile(i, k - 1))
                    if Tile(i, k - OUT_LAG).exists():
                        store(Tile(i, k - OUT_LAG))
                    if Tile(i, k + LEAD).exists():
                        load(Tile(i, k + LEAD))

            slots(0, range(BODY))
            slots(1, range(BODY))
            with sp.Fori(2, ITERS - 1) as i:
                slots(i, range(BODY))
            slots(ITERS - 1, range(BODY + OUT_LAG))
            for n in range(4):
                sp.wait_ge(o_st[n], 16 * (NT // 4))

        @block.gpsimd
        def _(pool):
            nc.gpsimd.memset(pad_end[:, 0, :], FAR).then_inc(pool_c, 1)
            nc.gpsimd.memset(pad_end[:, 1, :], 0).then_inc(pool_c, 1)
            nc.gpsimd.iota(base_i[:, :], pattern=[[TR * P, TG]], base=0, channel_multiplier=P)
            nc.gpsimd.iota(brow_i[:, :], pattern=[[P, NT]], base=0, channel_multiplier=0)
            nc.gpsimd.iota(iota_i[:, :], pattern=[[1, P]], base=0, channel_multiplier=0)
            nc.gpsimd.memset(neg_half[:, :], -0.5)
            nc.gpsimd.memset(ident[:, :], 0.0).then_inc(pool_c, 1)
            pool.wait_ge(pool_c, 3)
            nc.gpsimd.affine_select(out=ident[:, :], in_=ident[:, :], compare_op=ALU.not_equal, fill=1.0, base=0,
                                    pattern=[[-1, P]], channel_multiplier=1).then_inc(pool_c, 1)
            pool.wait_ge(dve_c, 5)
            for g in range(TG):
                nc.gpsimd.indirect_dma_start(row_dst_i[:, g, :], None, edge_rows,
                                             bass.IndirectOffsetOnAxis(ap=row_i[:, g:g + 1], axis=0),
                                             bounds_check=ROWS - 1, oob_is_err=False).then_inc(rows_in, 16)
            pool.wait_ge(padded, 64)
            pool.wait_ge(dve_c, 7)
            for g in range(TG):
                for pad, win, n in ((dst_pad, win_dst_i, WIN), (src_pad, win_src_i, P)):
                    table = pad[:, 0:(E + PAD) // n * n].rearrange("o (a b) -> (o a) b", b=n)
                    nc.gpsimd.indirect_dma_start(win[:, g, :], None, table,
                                                 bass.IndirectOffsetOnAxis(ap=start_i[:, g:g + 1], axis=1)).then_inc(wins_in, 16)
            pool.wait_ge(*ready)

            def copy_idx(t):
                nc.gpsimd.tensor_copy(idx[:, t.ring(8):t.ring(8) + 4],
                                      idx_c[:, bass.ds(t.i * BODY + t.off, 4)]).then_inc(idx_cp, 1)

            def gather(t):
                nc.gpsimd.indirect_dma_start(g_in[:, t.ring(4), :], None, x,
                                             bass.IndirectOffsetOnAxis(ap=idx[:, t.ring(8):t.ring(8) + 1], axis=0),
                                             bounds_check=N - 1, oob_is_err=False).then_inc(g_ld[t.ring(4)], 16)

            def gather_may(t):
                pool.wait_ge(idx_cp, t.quads())
                if t.off % 4 == 3:
                    wait(pool, g_ld[3], t.turns(4, back=1) * 16)

            def invert_std(t):
                pool.wait_ge(veps_done, t.count())
                wait(pool, hn_done, t.count(back=2))
                wait(pool, he_done, t.count(back=2))
                nc.gpsimd.tensor_tensor(rstd[:, t.ring(2), :], veps[:, t.ring(2), :], neg_half[:, :],
                                        ALU.pow).then_inc(rstd_done, 1)

            def times_v1(t):
                pool.wait_ge(he_done, t.count())
                wait(pool, a1_done, t.count(back=2))
                nc.gpsimd.tensor_tensor(prod[:, t.ring(2), :], he[:, t.ring(8), :], v1[:, :],
                                        ALU.mult).then_inc(prod_done, 1)

            def weigh(t):
                pool.wait_ge(alpha_sb, t.quads())
                pool.wait_ge(prod_done, t.count())
                rows = he[:, t.ring(8), :].rearrange("p (h d) -> p h d", h=H)
                by_head = alpha[:, t.off // QUAD % 2, t.off % QUAD, 0:H].unsqueeze(2).broadcast_to([P, H, D])
                nc.gpsimd.tensor_tensor(rows, rows, by_head, ALU.mult).then_inc(scaled, 1)

            copy_idx(Tile(0, 0))
            pool.wait_ge(idx_cp, 1)
            for k in range(LEAD):
                gather(Tile(0, k))
            invert_std(Tile(0, 0))
            pool.wait_ge(ld_v1, 32)

            def slots(i, ks):
                for k in ks:
                    ahead = Tile(i, k + LEAD)
                    if ahead.exists():
                        gather_may(ahead)
                    if Tile(i, k + 1).exists():
                        invert_std(Tile(i, k + 1))
                    if ahead.exists():
                        gather(ahead)
                    if ahead.off % 4 == 3 and Tile(i, k + LEAD + 1).exists():
                        copy_idx(Tile(i, k + LEAD + 1))
                    if Tile(i, k).exists():
                        times_v1(Tile(i, k))
                    if Tile(i, k - AGG_LAG).exists():
                        weigh(Tile(i, k - AGG_LAG))

            slots(0, range(BODY))
            slots(1, range(BODY))
            with pool.Fori(2, ITERS - 1) as i:
                slots(i, range(BODY))
            slots(ITERS - 1, range(BODY + AGG_LAG))

        @block.scalar
        def _(act):
            def normalise(t):
                r = t.ring(2)
                act.wait_ge(x_ld[t.ring(8)], t.turns(8) * 16)
                act.wait_ge(rstd_done, t.count())
                act.wait_ge(shift_done, t.count())
                wait(act, t_done, t.count(back=2) * 2)
                nc.scalar.activation(hn[:, r, :], x_in[:, t.ring(8), :], ACT.Relu, bias=shift[:, r, 0:1],
                                     scale=rstd[:, r, 0:1]).then_inc(hn_done, 1)
                act.wait_ge(g_ld[t.ring(4)], t.turns(4) * 16)
                wait(act, g_mm, t.count(back=8) * 2)
                nc.scalar.activation(he[:, t.ring(8), :], g_in[:, t.ring(4), :], ACT.Relu, bias=shift[:, r, 1:2],
                                     scale=rstd[:, r, 1:2]).then_inc(he_done, 1)

            def keep_transposes(t):
                wait(act, out_mm, t.count(back=8) * 2)
                act.wait_ge(t_done, t.count() * 2 - 1)
                nc.scalar.copy(hT[:, t.ring(8), 0:HALF], tp[:, 0, 0:HALF]).then_inc(hT_done, 1)
                act.wait_ge(t_done, t.count() * 2)
                nc.scalar.copy(hT[:, t.ring(8), HALF:F + P], tp[:, 1, :]).then_inc(hT_done, 1)

            def keep_sums(t):
                wait(act, out_mm, t.count(back=2) * 2)
                for half in range(2):
                    act.wait_ge(g_mm, t.count() * 2 - 1 + half)
                    nc.scalar.copy(gT[:, t.ring(2), HALF * half:HALF * half + HALF],
                                   gp[:, half, 0:HALF]).then_inc(gT_done, 1)

            def slots(i, ks):
                for k in ks:
                    t, last, agg = Tile(i, k), Tile(i, k - 1), Tile(i, k - AGG_LAG)
                    soft_now = k % QUAD == 0 and last.exists()
                    if soft_now:
                        act.wait_ge(a2_tr, last.quads())
                        wait(act, z_mm, last.quads(back=1))
                        nc.scalar.copy(a2[:, :], a2_ps).then_inc(a2_sb, 1)
                    if t.exists():
                        normalise(t)
                    if soft_now:
                        act.wait_ge(z_mm, last.quads())
                        wait(act, soft, last.quads(back=1) * SOFT)
                        nc.scalar.copy(z[:, :], z_ps).then_inc(z_sb, 1)
                    if k % QUAD == 1 and Tile(i, k - 2).exists():
                        q = Tile(i, k - 2)
                        act.wait_ge(alpha_tr, q.quads())
                        wait(act, scaled, q.quads(back=2) * QUAD)
                        nc.scalar.copy(alpha[:, q.off // QUAD % 2, :, :].rearrange("p a b -> p (a b)"),
                                       alpha_ps).then_inc(alpha_sb, 1)
                    if t.exists():
                        keep_transposes(t)
                    if soft_now:
                        act.wait_ge(soft, last.quads(back=1) * SOFT + 4)
                        nc.scalar.activation(wt[:, :], m1[:, :], ACT.Exp).then_inc(exp_done, 1)
                    if agg.exists():
                        keep_sums(agg)

            slots(0, range(BODY))
            slots(1, range(BODY))
            with act.Fori(2, ITERS - 1) as i:
                slots(i, range(BODY))
            slots(ITERS - 1, range(BODY + AGG_LAG))

        @block.vector
        def _(dve):
            v = nc.vector
            steps = [0]

            def step(ins):
                steps[0] += 1
                ins.then_inc(dve_c, 1)
                dve.wait_ge(dve_c, steps[0])

            v.memset(w_bd[:, :], 0.0)
            v.memset(v2[:, :, :], 0.0)
            v.memset(ones[:, :], 1.0)
            v.memset(a1[:, :, :, :], 0.0)
            v.memset(g_in[:, :, :], 0.0)
            v.memset(seg[:, :, :, :], 0.0)
            v.memset(loc_c[:, :], -1.0)
            v.memset(idx_c[:, :], FAR)
            step(v.memset(wres_bd[:, :], 0.0))
            dve.wait_ge(pool_c, 3)
            v.tensor_copy(iota_row[:, :], iota_i[:, :])
            v.tensor_copy(base_c[:, :], base_i[:, :])
            step(v.tensor_copy(brow[:, :], brow_i[:, :]))
            v.tensor_scalar(brow_s[:, :], brow[:, :], float(FIRST_SHIFTED * P), float(-SHIFT), ALU.is_ge, ALU.mult)
            v.tensor_scalar(shift_c[:, :], base_c[:, :], float(FIRST_SHIFTED * P), float(-SHIFT), ALU.is_ge, ALU.mult)
            dve.wait_ge(ld_edges, 16)
            step(v.tensor_copy(row_first[:, :], rows_i[:, 0:1]))
            v.tensor_tensor(base_c[:, :], base_c[:, :], shift_c[:, :], ALU.add)
            v.tensor_tensor(brow[:, :], brow[:, :], brow_s[:, :], ALU.add).then_inc(bn_done, 1)
            dve.wait_ge(bn_done, 1)
            step(v.tensor_scalar(before[:, :], brow[:, :], row_first[:, 0:1], None, ALU.is_gt))
            dve.wait_ge(pe_c, 1)
            v.tensor_scalar(row_c[:, :], z_ps[0:TR, 0:TG], 1.0, 0.0, ALU.subtract, ALU.max).then_inc(bn_done, 1)
            dve.wait_ge(bn_done, 2)
            step(v.tensor_copy(row_i[:, :], row_c[:, :]))
            dve.wait_ge(rows_in, 16 * TG)
            step(v.tensor_copy(row_dst[:, :, :], row_dst_i[:, :, :]))
            for g in range(TG):
                last = v.tensor_scalar(below[:, g, :], row_dst[:, g, :], base_c[:, g:g + 1], None, ALU.is_lt)
            last.then_inc(bn_done, 1)
            dve.wait_ge(bn_done, 3)
            v.tensor_reduce(below_n[:, :], below[:, :, :], AX.X, ALU.add).then_inc(bn_done, 1)
            dve.wait_ge(bn_done, 4)
            v.scalar_tensor_tensor(start_c[:, :], row_c[:, :], float(ROW), below_n[:, :], ALU.mult, ALU.add).then_inc(bn_done, 1)
            dve.wait_ge(bn_done, 5)
            step(v.tensor_copy(start_i[:, :], start_c[:, :]))
            dve.wait_ge(pe_c, 2)
            for a in range(2):
                heads = v2[D * a:D * a + D, :, 0:H].rearrange("p q (r b) -> p q r b", b=2)
                for p in range(PAIRS):
                    v.tensor_copy(heads[:, p, p, a:a + 1], a2_ps[D * a:D * a + D, 2 * p + a:2 * p + a + 1])
            step(v.tensor_copy(v1_row[:, :], a2T_ps[0:H, 0:D]))
            dve.wait_ge(wins_in, 32 * TG)
            for g in range(TG):
                last = v.tensor_scalar(win_loc[:, g, :], win_dst_i[:, g, :], base_c[:, g:g + 1], None, ALU.subtract)
            last.then_inc(bn_done, 1)
            v.tensor_copy(win_src[:, :, :], win_src_i[:, :, :]).then_inc(bn_done, 1)
            dve.wait_ge(bn_done, 7)
            step(v.tensor_scalar(win_far[:, :, :], win_loc[:, :, 0:P], float(P), float(FAR), ALU.is_ge, ALU.mult))
            step(v.tensor_tensor(win_src[:, :, :], win_src[:, :, :], win_far[:, :, :], ALU.add))
            step(v.tensor_tensor(seg[:, :, 1, 1:P], win_loc[:, :, 1:P], win_loc[:, :, 0:P - 1], ALU.is_equal))
            step(v.tensor_scalar(seg[:, :, 0, :], seg[:, :, 1, :], 1.0, -LOW, ALU.subtract, ALU.mult))
            for g in range(TG):
                dve.wait_ge(pe_c, 3 + g)
                v.tensor_copy(loc_c[:, TR * g:TR * g + TR], tp[:, g % 2, 0:TR])
                last = v.tensor_copy(idx_c[:, TR * g:TR * g + TR], tp[:, g % 2, P:P + TR])
                if g < 2:
                    step(last)
            last.then_inc(dve_c, 1)
            dve.wait_ge(dve_c, 15)

            def copy_loc(t):
                wait(dve, oh_done, t.count(back=5))
                v.tensor_copy(loc[:, t.ring(8):t.ring(8) + 4],
                              loc_c[:, bass.ds(t.i * BODY + t.off, 4)]).then_inc(loc_cp, 1)

            def make_onehot(t):
                dve.wait_ge(loc_cp, t.quads())
                wait(dve, g_mm, t.count(back=8) * 2)
                wait(dve, t_done, t.count(back=8) * 2)
                v.tensor_scalar(onehot[:, t.ring(8), :], iota_row[:, :], loc[:, t.ring(8):t.ring(8) + 1], None,
                                ALU.is_equal).then_inc(oh_done, 1)

            def statistics(t):
                r = t.ring(2)
                dve.wait_ge(x_ld[t.ring(8)], t.turns(8) * 16)
                for half in range(2):
                    v.bn_stats(stats[:, r, half, :], x_in[:, t.ring(8), HALF * half:HALF * half + HALF])
                dve.wait_ge(g_ld[t.ring(4)], t.turns(4) * 16)
                for half in range(2):
                    last = v.bn_stats(stats[:, r, 2 + half, :], g_in[:, t.ring(4), HALF * half:HALF * half + HALF])
                last.then_inc(bn_done, 1)
                dve.wait_ge(bn_done, t.count() + 7)
                make_onehot(t)
                for kind in range(2):
                    last = v.bn_aggr(mv[:, r, kind, :], stats[:, r, 2 * kind:2 * kind + 2, :].rearrange("p a b -> p (a b)"))
                last.then_inc(mv_done, 1)
                dve.wait_ge(mv_done, t.count())
                wait(dve, rstd_done, t.count(back=2))
                v.tensor_scalar(veps[:, r, :], mv[:, r, :, 1], EPS, None, ALU.add).then_inc(veps_done, 1)

            def shifts(t):
                r = t.ring(2)
                dve.wait_ge(rstd_done, t.count())
                wait(dve, he_done, t.count(back=2))
                v.scalar_tensor_tensor(shift[:, r, :], mv[:, r, :, 0], -1.0, rstd[:, r, :], ALU.mult,
                                       ALU.mult).then_inc(shift_done, 1)

            def sum_heads(t):
                dve.wait_ge(prod_done, t.count())
                wait(dve, z_mm, t.quads(back=2))
                v.tensor_reduce(a1[:, t.off // QUAD % 2, t.off % QUAD, 0:H],
                                prod[:, t.ring(2), :].rearrange("p (h d) -> p h d", h=H), AX.X,
                                ALU.add).then_inc(a1_done, 1)

            def finish(t):
                wait(dve, o_st[t.ring(4)], t.turns(4, back=1) * 16)
                for half in range(2):
                    f = HALF * half
                    dve.wait_ge(out_mm, t.count() * 2 - 1 + half)
                    v.scalar_tensor_tensor(o[:, t.ring(4), f:f + HALF], op[:, half, 0:HALF], 0.0,
                                           x_in[:, t.ring(8), f:f + HALF], ALU.max, ALU.add).then_inc(o_done, 1)

            def keep_a2T(q):
                dve.wait_ge(a2T_mm, q.quads() * QUAD)
                wait(dve, a2_tr, q.quads(back=1))
                v.tensor_copy(a2T[:, :], a2T_ps).then_inc(a2T_sb, 1)

            def soft_step(q, n, ins):
                ins.then_inc(soft, 1)
                dve.wait_ge(soft, q.quads(back=1) * SOFT + n)

            def soft_max(q):
                par = q.off // QUAD % 2
                low = segq[:, par, 0, :]
                dve.wait_ge(z_sb, q.quads())
                soft_step(q, 1, v.scalar_tensor_tensor(score[:, :], z[:, :], SLOPE, z[:, :], ALU.mult, ALU.max))
                dve.wait_ge(seg_ld[par], (q.i * 1 + (q.off // BODY + 1)) * 16)
                wait(dve, exp_done, q.quads(back=1))
                soft_step(q, 2, v.tensor_tensor_scan(m1[:, :], low[:, 0:P], score[:, :], LOW, ALU.add, ALU.max))
                soft_step(q, 3, v.tensor_tensor_scan(m2[:, ::-1], low[:, 1:WIN][:, ::-1], m1[:, ::-1], LOW,
                                                     ALU.add, ALU.max))
                soft_step(q, 4, v.tensor_tensor(m1[:, :], score[:, :], m2[:, :], ALU.subtract))

            def soft_sum(q):
                par = q.off // QUAD % 2
                same = segq[:, par, 1, :]
                dve.wait_ge(exp_done, q.quads())
                soft_step(q, 5, v.tensor_tensor_scan(s1[:, :], same[:, 0:P], wt[:, :], 0.0, ALU.mult, ALU.add))
                soft_step(q, 6, v.tensor_tensor_scan(s2[:, ::-1], same[:, 1:WIN][:, ::-1], s1[:, ::-1], 0.0,
                                                     ALU.mult, ALU.max))
                soft_step(q, 7, v.tensor_scalar(s1[:, :], s2[:, :], DENOM_MIN, None, ALU.max))
                soft_step(q, 8, v.reciprocal(s2[:, :], s1[:, :]))
                wait(dve, alpha_tr, q.quads(back=1))
                soft_step(q, 9, v.tensor_tensor(alphaT[:, :], wt[:, :], s2[:, :], ALU.mult))

            copy_loc(Tile(0, 0))
            statistics(Tile(0, 0))
            shifts(Tile(0, 0))

            def slots(i, ks):
                for k in ks:
                    t, nxt, q, late = Tile(i, k), Tile(i, k + 1), Tile(i, k - 1), Tile(i, k - OUT_LAG)
                    soft_now = k % QUAD == 0 and q.exists()
                    if soft_now:
                        keep_a2T(q)
                    if nxt.exists():
                        if (k + 1) % 4 == 0:
                            copy_loc(nxt)
                        statistics(nxt)
                        shifts(nxt)
                    if late.exists():
                        finish(late)
                    if soft_now:
                        soft_max(q)
                    if t.exists():
                        sum_heads(t)
                    if soft_now:
                        soft_sum(q)

            slots(0, range(BODY))
            slots(1, range(BODY))
            with dve.Fori(2, ITERS - 1) as i:
                slots(i, range(BODY))
            slots(ITERS - 1, range(BODY + OUT_LAG))

        @block.tensor
        def _(pe):
            mm = nc.tensor.matmul
            pe.wait_ge(dve_c, 4)
            for g in range(TG):
                last = mm(z_ps[0:TR, g:g + 1], before[:, TR * g:TR * g + TR], ones[:, :], start=True, stop=True)
            last.then_inc(pe_c, 1)
            pe.wait_ge(ld_w, 16 * 8)
            pe.wait_ge(dve_c, 5)
            mm(a2T_ps[0:H, 0:D], al_t[:, :], w_twice[:, 0, :], start=True, stop=True)
            mm(a2_ps[:, 0:H], w_twice[:, :, :].rearrange("p a b -> p (a b)"), ar_t[:, :], start=True,
               stop=True).then_inc(pe_c, 1)
            pe.wait_ge(pool_c, 4)
            pe.wait_ge(dve_c, 10)
            for g in range(TG):
                if g >= 2:
                    pe.wait_ge(dve_c, 11 + g)
                nc.tensor.transpose(tp[:, g % 2, 0:TR], win_loc[:, g, 0:P], ident[0:TR, 0:TR])
                nc.tensor.transpose(tp[:, g % 2, P:P + TR], win_src[:, g, :], ident[0:TR, 0:TR]).then_inc(pe_c, 1)
            pe.wait_ge(*ready)

            def transposes(t):
                r = t.ring(2)
                pe.wait_ge(hn_done, t.count())
                wait(pe, hT_done, t.count(back=1) * 2 - 1)
                for p in range(3):
                    last = nc.tensor.transpose(tp[:, 0, P * p:P * p + P], hn[:, r, P * p:P * p + P], ident[:, :])
                last.then_inc(t_done, 1)
                wait(pe, hT_done, t.count(back=1) * 2)
                for p in range(3):
                    nc.tensor.transpose(tp[:, 1, P * p:P * p + P], hn[:, r, P * (3 + p):P * (3 + p) + P], ident[:, :])
                pe.wait_ge(oh_done, t.count())
                nc.tensor.transpose(tp[:, 1, HALF:HALF + P], onehot[:, t.ring(8), :], ident[:, :]).then_inc(t_done, 1)

            def project_a2(t):
                j = t.off % QUAD
                pe.wait_ge(hT_done, t.count() * 2)
                if j == 0:
                    wait(pe, a2T_sb, t.quads(back=1))
                for p in range(PAIRS):
                    last = mm(a2T_ps[32 * j:32 * j + 32, :], v2[:, p, :], hT[:, t.ring(8), P * p:P * p + P],
                              start=(p == 0), stop=(p == PAIRS - 1))
                last.then_inc(a2T_mm, 1)

            def aggregate(t):
                pe.wait_ge(scaled, t.count())
                for half in range(2):
                    wait(pe, gT_done, t.count(back=1) * 2 - 1 + half)
                    for p in range(3):
                        f = P * (3 * half + p)
                        last = mm(gp[:, half, P * p:P * p + P], he[:, t.ring(8), f:f + P], onehot[:, t.ring(8), :],
                                  start=True, stop=True)
                    last.then_inc(g_mm, 1)

            def output(t, half):
                wait(pe, o_done, t.count(back=1) * 2 - 1 + half)
                pe.wait_ge(gT_done, t.count() * 2 - 1 + half)
                for p in range(3):
                    f = HALF * half + P * p
                    into = op[:, half, P * p:P * p + P]
                    mm(into, hT[:, t.ring(8), f:f + P], wres_bd[:, :], start=True, stop=False)
                    last = mm(into, gT[:, t.ring(2), f:f + P], w_bd[:, :], start=False, stop=True)
                last.then_inc(out_mm, 1)

            def turn_a2(q):
                pe.wait_ge(a2T_sb, q.quads())
                wait(pe, alpha_sb, q.quads(back=1))
                nc.tensor.transpose(a2_ps, a2T[:, :], ident[:, :]).then_inc(a2_tr, 1)

            def sum_scores(q):
                pe.wait_ge(a2_sb, q.quads())
                pe.wait_ge(a1_done, q.quads() * QUAD)
                wait(pe, z_sb, q.quads(back=1))
                for j in range(QUAD):
                    slot = (q.off // QUAD * QUAD + j) % 8
                    mm(z_ps[32 * j:32 * j + 32, :], a2[:, 32 * j:32 * j + 32], hT[:, slot, F:F + P], start=True,
                       stop=False)
                    last = mm(z_ps[32 * j:32 * j + 32, :], a1[:, q.off // QUAD % 2, j, :], ident[:, :], start=False,
                              stop=True)
                last.then_inc(z_mm, 1)

            def turn_alpha(q):
                pe.wait_ge(soft, q.quads() * SOFT)
                wait(pe, alpha_sb, q.quads(back=1))
                nc.tensor.transpose(alpha_ps, alphaT[:, :], ident[:, :]).then_inc(alpha_tr, 1)

            def slots(i, ks):
                for k in ks:
                    t, q, agg, late = Tile(i, k), Tile(i, k - 1), Tile(i, k - AGG_LAG), Tile(i, k - OUT_LAG)
                    soft_now = k % QUAD == 0 and q.exists()
                    if k % QUAD == 1 and Tile(i, k - 2).exists():
                        if late.exists():
                            output(late, 0)
                        turn_alpha(Tile(i, k - 2))
                        if late.exists():
                            output(late, 1)
                    elif late.exists():
                        output(late, 0)
                        if soft_now:
                            turn_a2(q)
                        output(late, 1)
                    elif soft_now:
                        turn_a2(q)
                    if soft_now:
                        sum_scores(q)
                    if t.exists():
                        transposes(t)
                    if agg.exists():
                        aggregate(agg)
                    if t.exists():
                        project_a2(t)

            slots(0, range(BODY))
            slots(1, range(BODY))
            with pe.Fori(2, ITERS - 1) as i:
                slots(i, range(BODY))
            slots(ITERS - 1, range(BODY + OUT_LAG))


def kernel(**inputs):
    import numpy as _np
    import concourse.bacc as _bacc
    from concourse import mybir as _mybir
    from concourse.bass_utils import run_bass_kernel_spmd as _run

    nc = _bacc.Bacc("TRN2", target_bir_lowering=False, num_devices=1)
    w, w_res = _np.asarray(inputs["L0_gnn_W"]), _np.asarray(inputs["L0_gnn_W_res"])
    laid_out = {
        "x": inputs["x"], "src": inputs["src"], "dst": inputs["dst"],
        "w_t": w.T, "w": w, "w_res_t": w_res.T,
        "attn_l_t": _np.asarray(inputs["L0_gnn_attn_l"])[0].T,
        "attn_r_t": _np.asarray(inputs["L0_gnn_attn_r"])[0].T,
    }
    arrays, args = {}, []
    for name, a in laid_out.items():
        a = _np.ascontiguousarray(a)
        arrays[f"in_{name}"] = a
        args.append(nc.dram_tensor(f"in_{name}", a.shape, _mybir.dt.from_np(a.dtype), kind="ExternalInput").ap())
    out = nc.dram_tensor("out_0", (N, F), FP32, kind="ExternalOutput").ap()
    gnn(nc, *args, out)
    r = _run(nc, [arrays], core_ids=[0])
    return r.results[0]["out_0"]
```

```python
import concourse.bass as bass
from concourse import mybir
from concourse.alu_op_type import AluOpType as ALU
from contextlib import ExitStack

FP32 = mybir.dt.float32
I32 = mybir.dt.int32
ACT = mybir.ActivationFunctionType
AX = mybir.AxisListType

N, F, E, H, D = 50000, 768, 25000, 12, 64
P = 128
PAIRS = F // P
HALF = F // 2
QUAD = 4
BODY = 16
NT = -(-N // (P * 8)) * 8
WHOLE = NT // BODY
LEFT = NT - WHOLE * BODY
SHIFTED = QUAD
SHIFT = NT * P - N
FIRST_SHIFTED = NT - SHIFTED
TG, TR = 4, NT // 4
ROWS, ROW = 125, E // 125
WIN = P + 1
PAD = 512
FAR = 1 << 20
LOW = -1.0e30
EPS = 1.0e-5
SLOPE = 0.2
DENOM_MIN = 1.0e-16
AGG_LAG = 6
OUT_LAG = 7
X_LEAD = 4
G_LEAD = 5
S_LEAD = 2


class Tile:

    def __init__(self, i, off):
        self.i, self.off = i, off

    def ring(self, n):
        return self.off % n

    def count(self, back=0):
        return self.i * BODY + (self.off + 1 - back)

    def turns(self, n, back=0):
        return self.i * (BODY // n) + (self.off // n + 1 - back)

    def quads(self, back=0):
        return self.i * (BODY // QUAD) + (self.off // QUAD + 1 - back)

    def exists(self):
        return not isinstance(self.i, int) or 0 <= self.i * BODY + self.off < NT

    def base(self):
        if isinstance(self.i, int):
            t = self.i * BODY + self.off
            return t * P - (SHIFT if t >= FIRST_SHIFTED else 0)
        return self.i * (BODY * P) + self.off * P


def wait(engine, sem, value):
    if not isinstance(value, int) or value > 0:
        engine.wait_ge(sem, value)


def gnn(nc, x, src, dst, w_t, w, w_res_t, attn_l_t, attn_r_t, out):
    ctx = ExitStack()
    with ctx:
        def sb(name, shape, dt=FP32):
            return ctx.enter_context(nc.sbuf_tensor(name, shape, dt))

        def ps(name, shape):
            return ctx.enter_context(nc.psum_tensor(name, shape, FP32))

        def sem(name):
            return ctx.enter_context(nc.semaphore(name))

        dst_pad = nc.dram_tensor("dst_pad", (1, E + PAD), I32, kind="Internal").ap()
        src_pad = nc.dram_tensor("src_pad", (1, E + PAD), I32, kind="Internal").ap()
        seg_dram = nc.dram_tensor("seg_dram", (NT, 2 * WIN), FP32, kind="Internal").ap()
        v1_dram = nc.dram_tensor("v1_dram", (H, D), FP32, kind="Internal").ap()

        ident = sb("ident", [P, P])
        iota_i = sb("iota_i", [P, P], I32)
        iota_row = sb("iota_row", [P, P])
        neg_half = sb("neg_half", [P, 2, 2])
        w_bd = sb("w_bd", [P, P])
        wres_bd = sb("wres_bd", [P, P])
        w_twice = sb("w_twice", [D, 2, D])
        al_t = sb("al_t", [D, H])
        ar_t = sb("ar_t", [D, H])
        v1_row = sb("v1_row", [H, D])
        v1 = sb("v1", [P, H * D])
        v2 = sb("v2", [P, PAIRS, 32])
        loc_c = sb("loc_c", [P, NT + BODY])
        idx_c = sb("idx_c", [P, NT + BODY], I32)
        base_i = sb("base_i", [TR, TG], I32)
        base_c = sb("base_c", [TR, TG])
        shift_c = sb("shift_c", [TR, TG])
        brow_i = sb("brow_i", [ROWS, NT], I32)
        brow = sb("brow", [ROWS, NT])
        brow_s = sb("brow_s", [ROWS, NT])
        rows_i = sb("rows_i", [ROWS, ROW], I32)
        row_first = sb("row_first", [ROWS, 1])
        before = sb("before", [ROWS, NT])
        ones = sb("ones", [ROWS, 1])
        row_c = sb("row_c", [TR, TG])
        row_i = sb("row_i", [TR, TG], I32)
        below_n = sb("below_n", [TR, TG])
        start_c = sb("start_c", [TR, TG])
        start_i = sb("start_i", [TR, TG], I32)
        seg = sb("seg", [TR, TG, 2, WIN])
        pad_end = sb("pad_end", [1, 2, PAD], I32)
        x_in = sb("x_in", [P, 16, F])
        g_in = sb("g_in", [P, 8, F])
        stats = sb("stats", [P, 4, 4, 6])
        mv = sb("mv", [P, 4, 2, 2])
        veps = sb("veps", [P, 4, 2])
        rstd = sb("rstd", [P, 4, 2])
        shift = sb("shift", [P, 4, 2])
        hn = sb("hn", [P, 2, F])
        he = sb("he", [P, 8, F])
        prod = sb("prod", [P, 2, F])
        wide = he[:, :, :].rearrange("p a b -> p (a b)")
        at, tables = 0, []
        for width, dt in ((ROW, I32), (ROW, FP32), (ROW, FP32), (WIN, I32), (P, I32), (WIN, FP32), (P, FP32), (P, FP32)):
            table = wide[0:TR, at:at + TG * width]
            tables.append((table if dt == FP32 else table.bitcast(dt)).rearrange("r (g c) -> r g c", g=TG))
            at += TG * width
        row_dst_i, row_dst, below, win_dst_i, win_src_i, win_loc, win_far, win_src = tables
        hT = sb("hT", [P, 8, F + P])
        gT = sb("gT", [P, 2, F])
        onehot = sb("onehot", [P, 16, P])
        o = sb("o", [P, 4, F])
        loc = sb("loc", [P, 8])
        idx = sb("idx", [P, 8], I32)
        a1 = sb("a1", [P, 2, QUAD, 32])
        a2T = sb("a2T", [P, P])
        a2 = sb("a2", [P, P])
        segq = sb("segq", [P, 2, 2, WIN])
        z = sb("z", [P, P])
        score = sb("score", [P, P])
        m1 = sb("m1", [P, P])
        m2 = sb("m2", [P, P])
        wt = sb("wt", [P, P])
        s1 = sb("s1", [P, P])
        s2 = sb("s2", [P, P])
        denom = sb("denom", [P, QUAD, H])
        rdenom = sb("rdenom", [P, QUAD, H])
        alpha = sb("alpha", [P, 2, QUAD, H])
        tp = ps("tp", [P, 2, 512])
        gp = ps("gp", [P, 2, 512])
        op = ps("op", [P, 2, 512])
        a2T_bank = ps("a2T_bank", [P, 512])
        soft_bank = ps("soft_bank", [P, 512])
        a2T_ps = a2T_bank[:, 0:P]
        a2_ps, z_ps, w_ps, s_ps = (soft_bank[:, P * n:P * n + P] for n in range(4))

        ld_edges = sem("ld_edges")
        ld_w = sem("ld_w")
        ld_v1 = sem("ld_v1")
        padded = sem("padded")
        rows_in = sem("rows_in")
        wins_in = sem("wins_in")
        seg_out = sem("seg_out")
        pool_c = sem("pool_c")
        dve_c = sem("dve_c")
        pe_c = sem("pe_c")
        x_ld = [sem(f"x_ld{n}") for n in range(16)]
        g_ld = [sem(f"g_ld{n}") for n in range(8)]
        o_st = [sem(f"o_st{n}") for n in range(4)]
        seg_ld = [sem(f"seg_ld{n}") for n in range(2)]
        idx_cp = sem("idx_cp")
        loc_cp = sem("loc_cp")
        bn_done = sem("bn_done")
        mv_done = sem("mv_done")
        veps_done = sem("veps_done")
        rstd_done = sem("rstd_done")
        shift_done = sem("shift_done")
        hn_done = sem("hn_done")
        he_done = sem("he_done")
        prod_done = sem("prod_done")
        a1_done = sem("a1_done")
        oh_done = sem("oh_done")
        t_done = sem("t_done")
        hT_done = sem("hT_done")
        a2T_mm = sem("a2T_mm")
        scaled = sem("scaled")
        g_mm = sem("g_mm")
        gT_done = sem("gT_done")
        out_mm = sem("out_mm")
        o_done = sem("o_done")
        a2T_sb = sem("a2T_sb")
        a2_tr = sem("a2_tr")
        a2_sb = sem("a2_sb")
        z_mm = sem("z_mm")
        z_sb = sem("z_sb")
        soft = sem("soft")
        exp_done = sem("exp_done")
        alpha_tr = sem("alpha_tr")
        SOFT = 6
        alpha_step = sem("alpha_step")

        block = ctx.enter_context(nc.Block())
        edge_rows = dst.rearrange("(a b) -> a b", b=ROW)
        ready = (dve_c, 15)

        @block.sync
        def _(sp):
            sp.dma_start(rows_i[:, :], edge_rows).then_inc(ld_edges, 16)
            sp.dma_start(dst_pad[:, 0:E], dst.rearrange("(o e) -> o e", o=1)).then_inc(padded, 16)
            sp.dma_start(src_pad[:, 0:E], src.rearrange("(o e) -> o e", o=1)).then_inc(padded, 16)
            sp.wait_ge(pool_c, 2)
            sp.dma_start(dst_pad[:, E:E + PAD], pad_end[:, 0, :]).then_inc(padded, 16)
            sp.dma_start(src_pad[:, E:E + PAD], pad_end[:, 1, :]).then_inc(padded, 16)
            sp.dma_start(w_twice[:, 0, :], w).then_inc(ld_w, 16)
            sp.dma_start(w_twice[:, 1, :], w).then_inc(ld_w, 16)
            sp.dma_start(al_t[:, :], attn_l_t).then_inc(ld_w, 16)
            sp.dma_start(ar_t[:, :], attn_r_t).then_inc(ld_w, 16)
            sp.wait_ge(dve_c, 1)
            for a in range(2):
                sp.dma_start(w_bd[D * a:D * a + D, D * a:D * a + D], w_t).then_inc(ld_w, 16)
                sp.dma_start(wres_bd[D * a:D * a + D, D * a:D * a + D], w_res_t).then_inc(ld_w, 16)

            def load(t):
                wait(sp, o_done, t.count(back=16) * 2)
                sp.dma_start(x_in[:, t.ring(16), :], x[bass.ds(t.base(), P), :]).then_inc(x_ld[t.ring(16)], 16)

            def load_flags(t):
                par = t.off // QUAD % 2
                wait(sp, soft, (t.quads(back=2)) * SOFT)
                first = t.i * BODY + t.off
                flags = seg_dram[bass.ds(first, QUAD), :]
                sp.dma_start(segq[:, par, :, :].rearrange("p a b -> p (a b)"),
                             flags.unsqueeze(1).broadcast_to([QUAD, 32, 2 * WIN])).then_inc(seg_ld[par], 16)

            def store(t):
                if isinstance(t.i, int) and t.i * BODY + t.off == FIRST_SHIFTED:
                    for n in range(4):
                        sp.wait_ge(o_st[n], t.turns(4, back=1) * 16)
                sp.wait_ge(o_done, t.count() * 2)
                sp.dma_start(out[bass.ds(t.base(), P), :], o[:, t.ring(4), :]).then_inc(o_st[t.ring(4)], 16)

            for k in range(X_LEAD):
                load(Tile(0, k))
            sp.wait_ge(dve_c, 8)
            sp.dma_start(v1_dram, v1_row[:, :]).then_inc(ld_v1, 16)
            sp.wait_ge(ld_v1, 16)
            sp.dma_start(v1[:, :], v1_dram.rearrange("(o h) d -> o (h d)", o=1).broadcast_to([P, H * D])).then_inc(ld_v1, 16)
            sp.wait_ge(*ready)
            sp.dma_start(seg_dram.rearrange("(g r) f -> r g f", g=TG),
                         seg[:, :, :, :].rearrange("r g a b -> r g (a b)")).then_inc(seg_out, 16)
            sp.wait_ge(seg_out, 16)

            def slots(i, ks):
                for k in ks:
                    if k % QUAD == 1 and Tile(i, k - 1).exists():
                        load_flags(Tile(i, k - 1))
                    if Tile(i, k - OUT_LAG).exists():
                        store(Tile(i, k - OUT_LAG))
                    if Tile(i, k + X_LEAD).exists():
                        load(Tile(i, k + X_LEAD))

            slots(0, range(BODY))
            with sp.Fori(1, WHOLE) as i:
                slots(i, range(BODY))
            slots(WHOLE, range(LEFT + OUT_LAG))
            for n in range(4):
                sp.wait_ge(o_st[n], 16 * (NT // 4))

        @block.gpsimd
        def _(pool):
            nc.gpsimd.memset(pad_end[:, 0, :], FAR).then_inc(pool_c, 1)
            nc.gpsimd.memset(pad_end[:, 1, :], 0).then_inc(pool_c, 1)
            nc.gpsimd.iota(base_i[:, :], pattern=[[TR * P, TG]], base=0, channel_multiplier=P)
            nc.gpsimd.iota(brow_i[:, :], pattern=[[P, NT]], base=0, channel_multiplier=0)
            nc.gpsimd.iota(iota_i[:, :], pattern=[[1, P]], base=0, channel_multiplier=0)
            nc.gpsimd.memset(neg_half[:, :, :], -0.5)
            nc.gpsimd.memset(ident[:, :], 0.0).then_inc(pool_c, 1)
            pool.wait_ge(pool_c, 3)
            nc.gpsimd.affine_select(out=ident[:, :], in_=ident[:, :], compare_op=ALU.not_equal, fill=1.0, base=0,
                                    pattern=[[-1, P]], channel_multiplier=1).then_inc(pool_c, 1)
            pool.wait_ge(dve_c, 5)
            for g in range(TG):
                nc.gpsimd.indirect_dma_start(row_dst_i[:, g, :], None, edge_rows,
                                             bass.IndirectOffsetOnAxis(ap=row_i[:, g:g + 1], axis=0),
                                             bounds_check=ROWS - 1, oob_is_err=False).then_inc(rows_in, 16)
            pool.wait_ge(padded, 64)
            pool.wait_ge(dve_c, 7)
            for g in range(TG):
                for pad, win, n in ((dst_pad, win_dst_i, WIN), (src_pad, win_src_i, P)):
                    table = pad[:, 0:(E + PAD) // n * n].rearrange("o (a b) -> (o a) b", b=n)
                    nc.gpsimd.indirect_dma_start(win[:, g, :], None, table,
                                                 bass.IndirectOffsetOnAxis(ap=start_i[:, g:g + 1], axis=1)).then_inc(wins_in, 16)
            pool.wait_ge(*ready)

            def copy_idx(t):
                nc.gpsimd.tensor_copy(idx[:, t.ring(8):t.ring(8) + 4],
                                      idx_c[:, bass.ds(t.i * BODY + t.off, 4)]).then_inc(idx_cp, 1)

            def gather(t):
                nc.gpsimd.indirect_dma_start(g_in[:, t.ring(8), :], None, x,
                                             bass.IndirectOffsetOnAxis(ap=idx[:, t.ring(8):t.ring(8) + 1], axis=0),
                                             bounds_check=N - 1, oob_is_err=False).then_inc(g_ld[t.ring(8)], 16)

            def gather_may(t):
                pool.wait_ge(idx_cp, t.quads())
                wait(pool, he_done, t.count(back=8))
                if t.off % 4 == 3:
                    last = Tile(t.i, t.off - 4)
                    wait(pool, g_ld[last.ring(8)], last.turns(8) * 16)

            def invert_std(t):
                r = t.ring(4)
                pool.wait_ge(veps_done, t.turns(2))
                wait(pool, hn_done, t.count(back=4))
                wait(pool, he_done, t.count(back=4))
                nc.gpsimd.tensor_tensor(rstd[:, r - 1:r + 1, :], veps[:, r - 1:r + 1, :], neg_half[:, :, :],
                                        ALU.pow).then_inc(rstd_done, 1)

            def times_v1(t):
                pool.wait_ge(he_done, t.count())
                wait(pool, a1_done, t.count(back=2))
                nc.gpsimd.tensor_tensor(prod[:, t.ring(2), :], he[:, t.ring(8), :], v1[:, :],
                                        ALU.mult).then_inc(prod_done, 1)

            def weigh(t):
                pool.wait_ge(alpha_step, t.quads() * 3)
                pool.wait_ge(prod_done, t.count())
                rows = he[:, t.ring(8), :].rearrange("p (h d) -> p h d", h=H)
                by_head = alpha[:, t.off // QUAD % 2, t.off % QUAD, :].unsqueeze(2).broadcast_to([P, H, D])
                nc.gpsimd.tensor_tensor(rows, rows, by_head, ALU.mult).then_inc(scaled, 1)

            copy_idx(Tile(0, 0))
            copy_idx(Tile(0, 4))
            pool.wait_ge(idx_cp, 2)
            for k in range(G_LEAD):
                gather(Tile(0, k))
            invert_std(Tile(0, 1))
            pool.wait_ge(ld_v1, 32)

            def slots(i, ks):
                for k in ks:
                    ahead = Tile(i, k + G_LEAD)
                    if ahead.exists():
                        gather_may(ahead)
                    if Tile(i, k - AGG_LAG).exists():
                        weigh(Tile(i, k - AGG_LAG))
                    if Tile(i, k).exists():
                        times_v1(Tile(i, k))
                    if k % 2 and Tile(i, k + S_LEAD).exists():
                        invert_std(Tile(i, k + S_LEAD))
                    if ahead.exists():
                        gather(ahead)
                    if ahead.off % 4 == 3 and Tile(i, ahead.off + 1).exists():
                        copy_idx(Tile(i, ahead.off + 1))

            slots(0, range(BODY))
            with pool.Fori(1, WHOLE) as i:
                slots(i, range(BODY))
            slots(WHOLE, range(LEFT + AGG_LAG))

        @block.scalar
        def _(act):
            def normalise(t):
                r, two = t.ring(4), t.ring(2)
                act.wait_ge(x_ld[t.ring(16)], t.turns(16) * 16)
                act.wait_ge(rstd_done, t.turns(2))
                act.wait_ge(shift_done, t.turns(2))
                wait(act, t_done, t.count(back=2) * 2)
                nc.scalar.activation(hn[:, two, :], x_in[:, t.ring(16), :], ACT.Relu, bias=shift[:, r, 0:1],
                                     scale=rstd[:, r, 0:1]).then_inc(hn_done, 1)

            def normalise_slots(t):
                r = t.ring(4)
                act.wait_ge(g_ld[t.ring(8)], t.turns(8) * 16)
                wait(act, g_mm, t.count(back=8) * 2)
                nc.scalar.activation(he[:, t.ring(8), :], g_in[:, t.ring(8), :], ACT.Relu, bias=shift[:, r, 1:2],
                                     scale=rstd[:, r, 1:2]).then_inc(he_done, 1)

            def keep_transposes(t):
                wait(act, out_mm, t.count(back=8) * 2)
                act.wait_ge(t_done, t.count() * 2 - 1)
                nc.scalar.copy(hT[:, t.ring(8), 0:HALF], tp[:, 0, 0:HALF]).then_inc(hT_done, 1)
                act.wait_ge(t_done, t.count() * 2)
                nc.scalar.copy(hT[:, t.ring(8), HALF:F + P], tp[:, 1, :]).then_inc(hT_done, 1)

            def keep_sums(t):
                wait(act, out_mm, t.count(back=2) * 2)
                for half in range(2):
                    act.wait_ge(g_mm, t.count() * 2 - 1 + half)
                    nc.scalar.copy(gT[:, t.ring(2), HALF * half:HALF * half + HALF],
                                   gp[:, half, 0:HALF]).then_inc(gT_done, 1)

            def slots(i, ks):
                for k in ks:
                    t, last, agg = Tile(i, k), Tile(i, k - 1), Tile(i, k - AGG_LAG)
                    soft_now = k % QUAD == 0 and last.exists()
                    if t.exists():
                        normalise(t)
                    if soft_now:
                        act.wait_ge(a2_tr, last.quads())
                        wait(act, z_mm, last.quads(back=1))
                        nc.scalar.copy(a2[:, :], a2_ps).then_inc(a2_sb, 1)
                    if t.exists():
                        normalise_slots(t)
                    if soft_now:
                        act.wait_ge(z_mm, last.quads())
                        wait(act, soft, last.quads(back=1) * SOFT)
                        nc.scalar.copy(z[:, :], z_ps).then_inc(z_sb, 1)
                    if t.exists():
                        keep_transposes(t)
                    if soft_now:
                        act.wait_ge(soft, last.quads(back=1) * SOFT + 4)
                        wait(act, alpha_tr, last.quads(back=1))
                        nc.scalar.activation(wt[:, :], m1[:, :], ACT.Exp).then_inc(exp_done, 1)
                    if agg.exists():
                        keep_sums(agg)

            slots(0, range(BODY))
            with act.Fori(1, WHOLE) as i:
                slots(i, range(BODY))
            slots(WHOLE, range(LEFT + AGG_LAG))

        @block.vector
        def _(dve):
            v = nc.vector
            steps = [0]

            def step(ins):
                steps[0] += 1
                ins.then_inc(dve_c, 1)
                dve.wait_ge(dve_c, steps[0])

            v.memset(w_bd[:, :], 0.0)
            v.memset(v2[:, :, :], 0.0)
            v.memset(ones[:, :], 1.0)
            v.memset(a1[:, :, :, :], 0.0)
            v.memset(g_in[:, :, :], 0.0)
            v.memset(seg[:, :, :, :], 0.0)
            v.memset(loc_c[:, :], -1.0)
            v.memset(idx_c[:, :], FAR)
            step(v.memset(wres_bd[:, :], 0.0))
            dve.wait_ge(pool_c, 3)
            v.tensor_copy(iota_row[:, :], iota_i[:, :])
            v.tensor_copy(base_c[:, :], base_i[:, :])
            step(v.tensor_copy(brow[:, :], brow_i[:, :]))
            v.tensor_scalar(brow_s[:, :], brow[:, :], float(FIRST_SHIFTED * P), float(-SHIFT), ALU.is_ge, ALU.mult)
            v.tensor_scalar(shift_c[:, :], base_c[:, :], float(FIRST_SHIFTED * P), float(-SHIFT), ALU.is_ge, ALU.mult)
            dve.wait_ge(ld_edges, 16)
            step(v.tensor_copy(row_first[:, :], rows_i[:, 0:1]))
            v.tensor_tensor(base_c[:, :], base_c[:, :], shift_c[:, :], ALU.add)
            v.tensor_tensor(brow[:, :], brow[:, :], brow_s[:, :], ALU.add).then_inc(bn_done, 1)
            dve.wait_ge(bn_done, 1)
            step(v.tensor_scalar(before[:, :], brow[:, :], row_first[:, 0:1], None, ALU.is_gt))
            dve.wait_ge(pe_c, 1)
            v.tensor_scalar(row_c[:, :], z_ps[0:TR, 0:TG], 1.0, 0.0, ALU.subtract, ALU.max).then_inc(bn_done, 1)
            dve.wait_ge(bn_done, 2)
            step(v.tensor_copy(row_i[:, :], row_c[:, :]))
            dve.wait_ge(rows_in, 16 * TG)
            step(v.tensor_copy(row_dst[:, :, :], row_dst_i[:, :, :]))
            for g in range(TG):
                last = v.tensor_scalar(below[:, g, :], row_dst[:, g, :], base_c[:, g:g + 1], None, ALU.is_lt)
            last.then_inc(bn_done, 1)
            dve.wait_ge(bn_done, 3)
            v.tensor_reduce(below_n[:, :], below[:, :, :], AX.X, ALU.add).then_inc(bn_done, 1)
            dve.wait_ge(bn_done, 4)
            v.scalar_tensor_tensor(start_c[:, :], row_c[:, :], float(ROW), below_n[:, :], ALU.mult, ALU.add).then_inc(bn_done, 1)
            dve.wait_ge(bn_done, 5)
            step(v.tensor_copy(start_i[:, :], start_c[:, :]))
            dve.wait_ge(pe_c, 2)
            for a in range(2):
                heads = v2[D * a:D * a + D, :, 0:H].rearrange("p q (r b) -> p q r b", b=2)
                for p in range(PAIRS):
                    v.tensor_copy(heads[:, p, p, a:a + 1], a2_ps[D * a:D * a + D, 2 * p + a:2 * p + a + 1])
            step(v.tensor_copy(v1_row[:, :], a2T_ps[0:H, 0:D]))
            dve.wait_ge(wins_in, 32 * TG)
            for g in range(TG):
                last = v.tensor_scalar(win_loc[:, g, :], win_dst_i[:, g, :], base_c[:, g:g + 1], None, ALU.subtract)
            last.then_inc(bn_done, 1)
            v.tensor_copy(win_src[:, :, :], win_src_i[:, :, :]).then_inc(bn_done, 1)
            dve.wait_ge(bn_done, 7)
            step(v.tensor_scalar(win_far[:, :, :], win_loc[:, :, 0:P], float(P), float(FAR), ALU.is_ge, ALU.mult))
            step(v.tensor_tensor(win_src[:, :, :], win_src[:, :, :], win_far[:, :, :], ALU.add))
            step(v.tensor_tensor(seg[:, :, 1, 1:P], win_loc[:, :, 1:P], win_loc[:, :, 0:P - 1], ALU.is_equal))
            step(v.tensor_scalar(seg[:, :, 0, :], seg[:, :, 1, :], 1.0, -LOW, ALU.subtract, ALU.mult))
            for g in range(TG):
                dve.wait_ge(pe_c, 3 + g)
                v.tensor_copy(loc_c[:, TR * g:TR * g + TR], tp[:, g % 2, 0:TR])
                last = v.tensor_copy(idx_c[:, TR * g:TR * g + TR], tp[:, g % 2, P:P + TR])
                if g < 2:
                    step(last)
            last.then_inc(dve_c, 1)
            dve.wait_ge(dve_c, 15)

            def copy_loc(t):
                wait(dve, oh_done, t.count(back=5))
                v.tensor_copy(loc[:, t.ring(8):t.ring(8) + 4],
                              loc_c[:, bass.ds(t.i * BODY + t.off, 4)]).then_inc(loc_cp, 1)

            def make_onehot(t):
                dve.wait_ge(loc_cp, t.quads())
                wait(dve, g_mm, t.count(back=16) * 2)
                wait(dve, t_done, t.count(back=16) * 2)
                v.tensor_scalar(onehot[:, t.ring(16), :], iota_row[:, :], loc[:, t.ring(8):t.ring(8) + 1], None,
                                ALU.is_equal).then_inc(oh_done, 1)

            def statistics(t):
                r = t.ring(4)
                dve.wait_ge(x_ld[t.ring(16)], t.turns(16) * 16)
                for half in range(2):
                    v.bn_stats(stats[:, r, half, :], x_in[:, t.ring(16), HALF * half:HALF * half + HALF])
                dve.wait_ge(g_ld[t.ring(8)], t.turns(8) * 16)
                for half in range(2):
                    last = v.bn_stats(stats[:, r, 2 + half, :], g_in[:, t.ring(8), HALF * half:HALF * half + HALF])
                last.then_inc(bn_done, 1)
                dve.wait_ge(bn_done, t.count() + 7)
                wait(dve, shift_done, t.turns(2, back=2))
                make_onehot(t)
                for kind in range(2):
                    last = v.bn_aggr(mv[:, r, kind, :], stats[:, r, 2 * kind:2 * kind + 2, :].rearrange("p a b -> p (a b)"))
                last.then_inc(mv_done, 1)

            def add_eps(t):
                r = t.ring(4)
                dve.wait_ge(mv_done, t.count())
                wait(dve, rstd_done, t.turns(2, back=2))
                v.tensor_scalar(veps[:, r - 1:r + 1, :], mv[:, r - 1:r + 1, :, 1], EPS, None, ALU.add).then_inc(veps_done, 1)

            def shifts(t):
                r = t.ring(4)
                dve.wait_ge(rstd_done, t.turns(2))
                wait(dve, he_done, t.count(back=4))
                wait(dve, hn_done, t.count(back=4))
                v.scalar_tensor_tensor(shift[:, r - 1:r + 1, :], mv[:, r - 1:r + 1, :, 0], -1.0, rstd[:, r - 1:r + 1, :],
                                       ALU.mult, ALU.mult).then_inc(shift_done, 1)

            def sum_heads(t):
                dve.wait_ge(prod_done, t.count())
                wait(dve, z_mm, t.quads(back=2))
                v.tensor_reduce(a1[:, t.off // QUAD % 2, t.off % QUAD, 0:H],
                                prod[:, t.ring(2), :].rearrange("p (h d) -> p h d", h=H), AX.X,
                                ALU.add).then_inc(a1_done, 1)

            def finish(t):
                wait(dve, o_st[t.ring(4)], t.turns(4, back=1) * 16)
                for half in range(2):
                    f = HALF * half
                    dve.wait_ge(out_mm, t.count() * 2 - 1 + half)
                    v.scalar_tensor_tensor(o[:, t.ring(4), f:f + HALF], op[:, half, 0:HALF], 0.0,
                                           x_in[:, t.ring(16), f:f + HALF], ALU.max, ALU.add).then_inc(o_done, 1)

            def keep_a2T(q):
                dve.wait_ge(a2T_mm, q.quads() * QUAD)
                wait(dve, a2_tr, q.quads(back=1))
                v.tensor_copy(a2T[:, :], a2T_ps).then_inc(a2T_sb, 1)

            def soft_step(q, n, ins):
                ins.then_inc(soft, 1)
                dve.wait_ge(soft, q.quads(back=1) * SOFT + n)

            def soft_max(q):
                par = q.off // QUAD % 2
                low = segq[:, par, 0, :]
                dve.wait_ge(z_sb, q.quads())
                soft_step(q, 1, v.scalar_tensor_tensor(score[:, :], z[:, :], SLOPE, z[:, :], ALU.mult, ALU.max))
                dve.wait_ge(seg_ld[par], q.turns(8) * 16)
                soft_step(q, 2, v.tensor_tensor_scan(m1[:, :], low[:, 0:P], score[:, :], LOW, ALU.add, ALU.max))
                soft_step(q, 3, v.tensor_tensor_scan(m2[:, ::-1], low[:, 1:WIN][:, ::-1], m1[:, ::-1], LOW,
                                                     ALU.add, ALU.max))
                soft_step(q, 4, v.tensor_tensor(m1[:, :], score[:, :], m2[:, :], ALU.subtract))

            def soft_sum(q):
                par = q.off // QUAD % 2
                same = segq[:, par, 1, :]
                dve.wait_ge(exp_done, q.quads())
                soft_step(q, 5, v.tensor_tensor_scan(s1[:, :], same[:, 0:P], wt[:, :], 0.0, ALU.mult, ALU.add))
                wait(dve, alpha_tr, q.quads(back=1))
                soft_step(q, 6, v.tensor_tensor_scan(s2[:, ::-1], same[:, 1:WIN][:, ::-1], s1[:, ::-1], 0.0,
                                                     ALU.mult, ALU.max))

            def alphas(q):
                par = q.off // QUAD % 2
                of_slot = lambda bank: bank.rearrange("p (a b) -> p a b", b=32)[:, :, 0:H]
                dve.wait_ge(alpha_tr, q.quads())
                v.tensor_scalar(denom[:, :, :], of_slot(s_ps), DENOM_MIN, None, ALU.max).then_inc(alpha_step, 1)
                dve.wait_ge(alpha_step, q.quads(back=1) * 3 + 1)
                v.reciprocal(rdenom[:, :, :], denom[:, :, :]).then_inc(alpha_step, 1)
                dve.wait_ge(alpha_step, q.quads(back=1) * 3 + 2)
                wait(dve, scaled, q.quads(back=2) * QUAD)
                v.tensor_tensor(alpha[:, par, :, :], of_slot(w_ps), rdenom[:, :, :], ALU.mult).then_inc(alpha_step, 1)

            copy_loc(Tile(0, 0))
            statistics(Tile(0, 0))
            statistics(Tile(0, 1))
            add_eps(Tile(0, 1))
            shifts(Tile(0, 1))

            def slots(i, ks):
                for k in ks:
                    t, nxt, q, late = Tile(i, k), Tile(i, k + S_LEAD), Tile(i, k - 1), Tile(i, k - OUT_LAG)
                    soft_now = k % QUAD == 0 and q.exists()
                    if soft_now:
                        keep_a2T(q)
                    if nxt.exists():
                        if nxt.off % 4 == 0:
                            copy_loc(nxt)
                        statistics(nxt)
                        if k % 2:
                            add_eps(nxt)
                    if late.exists():
                        finish(late)
                    if k % QUAD == 1 and Tile(i, k - 2).exists():
                        alphas(Tile(i, k - 2))
                    if soft_now:
                        soft_max(q)
                    if t.exists():
                        sum_heads(t)
                    if nxt.exists() and k % 2:
                        shifts(nxt)
                    if soft_now:
                        soft_sum(q)

            slots(0, range(BODY))
            with dve.Fori(1, WHOLE) as i:
                slots(i, range(BODY))
            slots(WHOLE, range(LEFT + OUT_LAG))

        @block.tensor
        def _(pe):
            mm = nc.tensor.matmul
            pe.wait_ge(dve_c, 4)
            for g in range(TG):
                last = mm(z_ps[0:TR, g:g + 1], before[:, TR * g:TR * g + TR], ones[:, :], start=True, stop=True)
            last.then_inc(pe_c, 1)
            pe.wait_ge(ld_w, 16 * 8)
            pe.wait_ge(dve_c, 5)
            mm(a2T_ps[0:H, 0:D], al_t[:, :], w_twice[:, 0, :], start=True, stop=True)
            mm(a2_ps[:, 0:H], w_twice[:, :, :].rearrange("p a b -> p (a b)"), ar_t[:, :], start=True,
               stop=True).then_inc(pe_c, 1)
            pe.wait_ge(pool_c, 4)
            pe.wait_ge(dve_c, 10)
            for g in range(TG):
                if g >= 2:
                    pe.wait_ge(dve_c, 11 + g)
                nc.tensor.transpose(tp[:, g % 2, 0:TR], win_loc[:, g, 0:P], ident[0:TR, 0:TR])
                nc.tensor.transpose(tp[:, g % 2, P:P + TR], win_src[:, g, :], ident[0:TR, 0:TR]).then_inc(pe_c, 1)
            pe.wait_ge(*ready)

            def transposes(t):
                r = t.ring(2)
                pe.wait_ge(hn_done, t.count())
                wait(pe, hT_done, t.count(back=1) * 2 - 1)
                for p in range(3):
                    last = nc.tensor.transpose(tp[:, 0, P * p:P * p + P], hn[:, r, P * p:P * p + P], ident[:, :])
                last.then_inc(t_done, 1)
                wait(pe, hT_done, t.count(back=1) * 2)
                for p in range(3):
                    nc.tensor.transpose(tp[:, 1, P * p:P * p + P], hn[:, r, P * (3 + p):P * (3 + p) + P], ident[:, :])
                pe.wait_ge(oh_done, t.count())
                nc.tensor.transpose(tp[:, 1, HALF:HALF + P], onehot[:, t.ring(16), :], ident[:, :]).then_inc(t_done, 1)

            def project_a2(t):
                j = t.off % QUAD
                pe.wait_ge(hT_done, t.count() * 2)
                if j == 0:
                    wait(pe, a2T_sb, t.quads(back=1))
                for p in range(PAIRS):
                    last = mm(a2T_ps[32 * j:32 * j + 32, :], v2[:, p, :], hT[:, t.ring(8), P * p:P * p + P],
                              start=(p == 0), stop=(p == PAIRS - 1))
                last.then_inc(a2T_mm, 1)

            def aggregate(t):
                pe.wait_ge(scaled, t.count())
                for half in range(2):
                    wait(pe, gT_done, t.count(back=1) * 2 - 1 + half)
                    for p in range(3):
                        f = P * (3 * half + p)
                        last = mm(gp[:, half, P * p:P * p + P], he[:, t.ring(8), f:f + P], onehot[:, t.ring(16), :],
                                  start=True, stop=True)
                    last.then_inc(g_mm, 1)

            def output(t, half):
                wait(pe, o_done, t.count(back=1) * 2 - 1 + half)
                pe.wait_ge(gT_done, t.count() * 2 - 1 + half)
                for p in range(3):
                    f = HALF * half + P * p
                    into = op[:, half, P * p:P * p + P]
                    mm(into, hT[:, t.ring(8), f:f + P], wres_bd[:, :], start=True, stop=False)
                    last = mm(into, gT[:, t.ring(2), f:f + P], w_bd[:, :], start=False, stop=True)
                last.then_inc(out_mm, 1)

            def turn_a2(q):
                pe.wait_ge(a2T_sb, q.quads())
                wait(pe, alpha_step, q.quads(back=1) * 3)
                nc.tensor.transpose(a2_ps, a2T[:, :], ident[:, :]).then_inc(a2_tr, 1)

            def sum_scores(q):
                pe.wait_ge(a2_sb, q.quads())
                pe.wait_ge(a1_done, q.quads() * QUAD)
                wait(pe, z_sb, q.quads(back=1))
                for j in range(QUAD):
                    slot = (q.off // QUAD * QUAD + j) % 8
                    mm(z_ps[32 * j:32 * j + 32, :], a2[:, 32 * j:32 * j + 32], hT[:, slot, F:F + P], start=True,
                       stop=False)
                    last = mm(z_ps[32 * j:32 * j + 32, :], a1[:, q.off // QUAD % 2, j, :], ident[:, :], start=False,
                              stop=True)
                last.then_inc(z_mm, 1)

            def turn_alpha(q):
                pe.wait_ge(soft, q.quads() * SOFT)
                nc.tensor.transpose(w_ps, wt[:, :], ident[:, :])
                nc.tensor.transpose(s_ps, s2[:, :], ident[:, :]).then_inc(alpha_tr, 1)

            def slots(i, ks):
                for k in ks:
                    t, q, agg, late = Tile(i, k), Tile(i, k - 1), Tile(i, k - AGG_LAG), Tile(i, k - OUT_LAG)
                    soft_now = k % QUAD == 0 and q.exists()
                    if k % QUAD == 1 and Tile(i, k - 2).exists():
                        if late.exists():
                            output(late, 0)
                        turn_alpha(Tile(i, k - 2))
                        if late.exists():
                            output(late, 1)
                    elif late.exists():
                        output(late, 0)
                        if soft_now:
                            turn_a2(q)
                        output(late, 1)
                    elif soft_now:
                        turn_a2(q)
                    if soft_now:
                        sum_scores(q)
                    if t.exists():
                        transposes(t)
                    if agg.exists():
                        aggregate(agg)
                    if t.exists():
                        project_a2(t)

            slots(0, range(BODY))
            with pe.Fori(1, WHOLE) as i:
                slots(i, range(BODY))
            slots(WHOLE, range(LEFT + OUT_LAG))


def kernel(**inputs):
    import numpy as _np
    import concourse.bacc as _bacc
    from concourse import mybir as _mybir
    from concourse.bass_utils import run_bass_kernel_spmd as _run

    nc = _bacc.Bacc("TRN2", target_bir_lowering=False, num_devices=1)
    w, w_res = _np.asarray(inputs["L0_gnn_W"]), _np.asarray(inputs["L0_gnn_W_res"])
    laid_out = {
        "x": inputs["x"], "src": inputs["src"], "dst": inputs["dst"],
        "w_t": w.T, "w": w, "w_res_t": w_res.T,
        "attn_l_t": _np.asarray(inputs["L0_gnn_attn_l"])[0].T,
        "attn_r_t": _np.asarray(inputs["L0_gnn_attn_r"])[0].T,
    }
    arrays, args = {}, []
    for name, a in laid_out.items():
        a = _np.ascontiguousarray(a)
        arrays[f"in_{name}"] = a
        args.append(nc.dram_tensor(f"in_{name}", a.shape, _mybir.dt.from_np(a.dtype), kind="ExternalInput").ap())
    out = nc.dram_tensor("out_0", (N, F), FP32, kind="ExternalOutput").ap()
    gnn(nc, *args, out)
    r = _run(nc, [arrays], core_ids=[0])
    return r.results[0]["out_0"]
```

```python
import concourse.bass as bass
from concourse import mybir
from concourse.alu_op_type import AluOpType as ALU
from contextlib import ExitStack

FP32 = mybir.dt.float32
I32 = mybir.dt.int32
ACT = mybir.ActivationFunctionType
AX = mybir.AxisListType

N, F, E, H, D = 50000, 768, 25000, 12, 64
P = 128
PAIRS = F // P
HALF = F // 2
QUAD = 4
BODY = 32
NT = -(-N // (P * 8)) * 8
WHOLE = NT // BODY
LEFT = NT - WHOLE * BODY
SHIFTED = QUAD
SHIFT = NT * P - N
FIRST_SHIFTED = NT - SHIFTED
TG, TR = 4, NT // 4
ROWS, ROW = 125, E // 125
WIN = P + 1
PAD = 512
FAR = 1 << 17
LOW = -1.0e30
EPS = 1.0e-5
SLOPE = 0.2
DENOM_MIN = 1.0e-16
AGG_LAG = 6
OUT_LAG = 7
X_LEAD = 4
G_LEAD = 5
S_LEAD = 2
EARLY = 4
FRESH = P - 1
CHUNKS = -(-E // FRESH)
STEPS = 24


class Tile:

    def __init__(self, i, off):
        self.i, self.off = i, off

    def ring(self, n):
        return self.off % n

    def count(self, back=0):
        return self.i * BODY + (self.off + 1 - back)

    def turns(self, n, back=0):
        return self.i * (BODY // n) + (self.off // n + 1 - back)

    def quads(self, back=0):
        return self.i * (BODY // QUAD) + (self.off // QUAD + 1 - back)

    def exists(self):
        return not isinstance(self.i, int) or 0 <= self.i * BODY + self.off < NT

    def base(self):
        if isinstance(self.i, int):
            t = self.i * BODY + self.off
            return t * P - (SHIFT if t >= FIRST_SHIFTED else 0)
        return self.i * (BODY * P) + self.off * P


def wait(engine, sem, value):
    if not isinstance(value, int) or value > 0:
        engine.wait_ge(sem, value)


def gnn(nc, x, edges, dst, w_t, w, w_res_t, attn_l_t, attn_r_t, out):
    ctx = ExitStack()
    with ctx:
        def sb(name, shape, dt=FP32):
            return ctx.enter_context(nc.sbuf_tensor(name, shape, dt))

        def ps(name, shape):
            return ctx.enter_context(nc.psum_tensor(name, shape, FP32))

        def sem(name):
            return ctx.enter_context(nc.semaphore(name))

        seg_dram = nc.dram_tensor("seg_dram", (NT, 2 * WIN), FP32, kind="Internal").ap()
        v1_dram = nc.dram_tensor("v1_dram", (H, D), FP32, kind="Internal").ap()
        carry_dram = nc.dram_tensor("carry_dram", (1, F + 2 * H), FP32, kind="Internal").ap()

        ident = sb("ident", [P, P])
        iota_i = sb("iota_i", [P, P], I32)
        iota_row = sb("iota_row", [P, P])
        neg_half = sb("neg_half", [P, 2, 2])
        w_bd = sb("w_bd", [P, P])
        wres_bd = sb("wres_bd", [P, P])
        w_twice = sb("w_twice", [D, 2, D])
        al_t = sb("al_t", [D, H])
        ar_t = sb("ar_t", [D, H])
        v1_row = sb("v1_row", [H, D])
        v1 = sb("v1", [P, H * D])
        v2 = sb("v2", [P, PAIRS, 32])
        loc_c = sb("loc_c", [P, NT + BODY])
        idx_c = sb("idx_c", [P, NT + BODY], I32)
        base_i = sb("base_i", [TR, TG], I32)
        base_c = sb("base_c", [TR, TG])
        shift_c = sb("shift_c", [TR, TG])
        brow_i = sb("brow_i", [ROWS, NT], I32)
        brow = sb("brow", [ROWS, NT])
        brow_s = sb("brow_s", [ROWS, NT])
        rows_i = sb("rows_i", [ROWS, ROW], I32)
        row_first = sb("row_first", [ROWS, 1])
        before = sb("before", [ROWS, NT])
        ones = sb("ones", [ROWS, 1])
        first_act = sb("first_act", [ROWS, 1])
        row_c = sb("row_c", [TR, TG])
        row_i = sb("row_i", [TR, TG], I32)
        below_n = sb("below_n", [TR, TG])
        start_c = sb("start_c", [TR, TG])
        start_i = sb("start_i", [TR, TG], I32)
        seg = sb("seg", [TR, TG, 2, WIN])
        crowded = sb("crowded", [TR, TG])
        crowded_n = sb("crowded_n", [TR, 1])
        crowded_i = sb("crowded_i", [1, 1], I32)
        x_in = sb("x_in", [P, 16, F])
        g_in = sb("g_in", [P, 8, F])
        stats = sb("stats", [P, 4, 4, 6])
        mv = sb("mv", [P, 4, 2, 2])
        veps = sb("veps", [P, 4, 2])
        rstd = sb("rstd", [P, 4, 2])
        shift = sb("shift", [P, 4, 2])
        hn = sb("hn", [P, 2, F])
        he = sb("he", [P, 8, F])
        prod = sb("prod", [P, 2, F])
        wide = he[:, :, :].rearrange("p a b -> p (a b)")
        at, tables = 0, []
        for width, dt in ((ROW, I32), (ROW, FP32), (ROW, FP32), (2 * WIN, I32), (WIN, FP32), (P, FP32), (P, FP32)):
            table = wide[0:TR, at:at + TG * width]
            tables.append((table if dt == FP32 else table.bitcast(dt)).rearrange("r (g c) -> r g c", g=TG))
            at += TG * width
        row_dst_i, row_dst, below, win_i, win_loc, win_far, win_src = tables
        win_pairs = win_i.rearrange("r g (e two) -> r g e two", two=2)
        hT = sb("hT", [P, 8, F + P])
        gT = sb("gT", [P, 2, F])
        onehot = sb("onehot", [P, 16, P])
        o = sb("o", [P, 4, F])
        loc = sb("loc", [P, 8])
        idx = sb("idx", [P, 8], I32)
        a1 = sb("a1", [P, 2, QUAD, 32])
        a2T = sb("a2T", [P, P])
        a2 = sb("a2", [P, P])
        segq = sb("segq", [P, 2, 2, WIN])
        z = sb("z", [P, P])
        score = sb("score", [P, P])
        m1 = sb("m1", [P, P])
        m2 = sb("m2", [P, P])
        wt = sb("wt", [P, P])
        s1 = sb("s1", [P, P])
        s2 = sb("s2", [P, P])
        denom = sb("denom", [P, QUAD, H])
        rdenom = sb("rdenom", [P, QUAD, H])
        alpha = sb("alpha", [P, 2, QUAD, H])
        rows = lambda n, count: x_in[:, n:n + count, :].rearrange("p a f -> p (a f)")
        c_src, c_dst = x_in[:, 0, :], x_in[:, 1, :]
        c_he, c_hd = x_in[:, 2, :], x_in[:, 3, :]
        c_prod = x_in[:, 4, :]
        c_sums = x_in[:, 5, :]
        c_out = x_in[:, 6, :]
        c_hdT, c_gT = x_in[:, 7, :], x_in[:, 8, :]
        c_masked = rows(9, 2)[:, 0:H * P].rearrange("p (h s) -> p h s", h=H)
        c_pick = rows(11, 2)[0:H, 0:H * P].rearrange("p (h s) -> p h s", h=H)
        c_same = x_in[:, 13, 0:P]
        c_low = x_in[:, 13, P:2 * P]
        c_row_dst = x_in[:, 13, 2 * P:3 * P]
        c_pairs = x_in[:, 13, 3 * P:5 * P].bitcast(I32)
        c_scoreT = x_in[0:H, 14, 0:P]
        c_apart = x_in[:, 14, P:2 * P]
        at, small = 0, []
        for width in (4, 4, 1, 1, 1, 24, 2, 2, 2, 4, 2, H, H, H, H, H, H, H, H, H, H, H):
            small.append(x_in[:, 15, at:at + width])
            at += width
        (c_cols, c_colf, c_more, c_to, c_to_i, c_stats, c_veps, c_rstd, c_shift, c_mv, c_idle, c_a1, c_z, c_score,
         c_max, c_diff, c_weight, c_factor, c_dweight, c_denom, c_dmin, c_rden) = small
        c_cols, c_to_i = c_cols.bitcast(I32), c_to_i.bitcast(I32)
        c_stats = c_stats.rearrange("p (a b) -> p a b", a=4)
        c_mv = c_mv.rearrange("p (a b) -> p a b", a=2)
        tp = ps("tp", [P, 2, 512])
        gp = ps("gp", [P, 2, 512])
        op = ps("op", [P, 2, 512])
        a2T_bank = ps("a2T_bank", [P, 512])
        soft_bank = ps("soft_bank", [P, 512])
        a2T_ps = a2T_bank[:, 0:P]
        a2_ps, z_ps, w_ps, s_ps = (soft_bank[:, P * n:P * n + P] for n in range(4))

        c_scoreT_ps, c_a2_ps, c_denom_ps = z_ps[0:H, :], w_ps[:, 0:H], s_ps[:, 0:H]
        spread_at = ((gp, 0), (gp, 1), (op, 0))

        ld_edges = sem("ld_edges")
        ld_w = sem("ld_w")
        ld_v1 = sem("ld_v1")
        rows_in = sem("rows_in")
        wins_in = sem("wins_in")
        seg_out = sem("seg_out")
        pool_c = sem("pool_c")
        dve_c = sem("dve_c")
        pe_c = sem("pe_c")
        c_ready = sem("c_ready")
        c_step = sem("c_step")
        c_carried = sem("c_carried")
        c_cols_in = sem("c_cols_in")
        c_apart_done = sem("c_apart_done")
        c_rows_in = sem("c_rows_in")
        c_rstd_done = sem("c_rstd_done")
        c_h_done = sem("c_h_done")
        c_exp_done = sem("c_exp_done")
        c_state_in = sem("c_state_in")
        c_pe = sem("c_pe")
        c_out_may = sem("c_out_may")
        c_rows_out = sem("c_rows_out")
        x_ld = [sem(f"x_ld{n}") for n in range(16)]
        g_ld = [sem(f"g_ld{n}") for n in range(8)]
        o_st = [sem(f"o_st{n}") for n in range(4)]
        seg_ld = [sem(f"seg_ld{n}") for n in range(2)]
        idx_cp = sem("idx_cp")
        loc_cp = sem("loc_cp")
        bn_done = sem("bn_done")
        mv_done = sem("mv_done")
        veps_done = sem("veps_done")
        rstd_done = sem("rstd_done")
        shift_done = sem("shift_done")
        hn_done = sem("hn_done")
        he_done = sem("he_done")
        prod_done = sem("prod_done")
        a1_done = sem("a1_done")
        oh_done = sem("oh_done")
        t_done = sem("t_done")
        hT_done = sem("hT_done")
        a2T_mm = sem("a2T_mm")
        scaled = sem("scaled")
        g_mm = sem("g_mm")
        gT_done = sem("gT_done")
        out_mm = sem("out_mm")
        o_done = sem("o_done")
        a2T_sb = sem("a2T_sb")
        a2_tr = sem("a2_tr")
        a2_sb = sem("a2_sb")
        z_mm = sem("z_mm")
        z_sb = sem("z_sb")
        soft = sem("soft")
        exp_done = sem("exp_done")
        alpha_tr = sem("alpha_tr")
        SOFT = 6
        alpha_step = sem("alpha_step")

        block = ctx.enter_context(nc.Block())
        edge_rows = dst.rearrange("(a b) -> a b", b=ROW)
        ready = (dve_c, 17)

        @block.sync
        def _(sp):
            sp.dma_start(rows_i[:, :], edge_rows).then_inc(ld_edges, 16)
            sp.dma_start(w_twice[:, 0, :], w).then_inc(ld_w, 16)
            sp.dma_start(w_twice[:, 1, :], w).then_inc(ld_w, 16)
            sp.dma_start(al_t[:, :], attn_l_t).then_inc(ld_w, 16)
            sp.dma_start(ar_t[:, :], attn_r_t).then_inc(ld_w, 16)
            sp.wait_ge(dve_c, 1)
            for a in range(2):
                sp.dma_start(w_bd[D * a:D * a + D, D * a:D * a + D], w_t).then_inc(ld_w, 16)
                sp.dma_start(wres_bd[D * a:D * a + D, D * a:D * a + D], w_res_t).then_inc(ld_w, 16)

            def load(t):
                wait(sp, o_done, t.count(back=16) * 2)
                sp.dma_start(x_in[:, t.ring(16), :], x[bass.ds(t.base(), P), :]).then_inc(x_ld[t.ring(16)], 16)

            def load_flags(t):
                par = t.off // QUAD % 2
                wait(sp, soft, (t.quads(back=2)) * SOFT)
                first = t.i * BODY + t.off
                flags = seg_dram[bass.ds(first, QUAD), :]
                sp.dma_start(segq[:, par, :, :].rearrange("p a b -> p (a b)"),
                             flags.unsqueeze(1).broadcast_to([QUAD, 32, 2 * WIN])).then_inc(seg_ld[par], 16)

            def store(t):
                if isinstance(t.i, int) and t.i * BODY + t.off == FIRST_SHIFTED:
                    for n in range(4):
                        sp.wait_ge(o_st[n], t.turns(4, back=1) * 16)
                sp.wait_ge(o_done, t.count() * 2)
                sp.dma_start(out[bass.ds(t.base(), P), :], o[:, t.ring(4), :]).then_inc(o_st[t.ring(4)], 16)

            for k in range(X_LEAD):
                load(Tile(0, k))
            sp.wait_ge(dve_c, 8)
            sp.dma_start(v1_dram, v1_row[:, :]).then_inc(ld_v1, 16)
            sp.wait_ge(ld_v1, 16)
            sp.dma_start(v1[:, :], v1_dram.rearrange("(o h) d -> o (h d)", o=1).broadcast_to([P, H * D])).then_inc(ld_v1, 16)
            sp.wait_ge(*ready)
            sp.dma_start(seg_dram.rearrange("(g r) f -> r g f", g=TG),
                         seg[:, :, :, :].rearrange("r g a b -> r g (a b)")).then_inc(seg_out, 16)
            sp.wait_ge(seg_out, 16)

            def slots(i, ks):
                for k in ks:
                    if k % QUAD == 1 and Tile(i, k - 1).exists():
                        load_flags(Tile(i, k - 1))
                    if Tile(i, k - OUT_LAG).exists():
                        store(Tile(i, k - OUT_LAG))
                    if Tile(i, k + X_LEAD).exists():
                        load(Tile(i, k + X_LEAD))

            slots(0, range(BODY))
            with sp.Fori(1, WHOLE) as i:
                slots(i, range(BODY))
            slots(WHOLE, range(LEFT + OUT_LAG))
            for n in range(4):
                sp.wait_ge(o_st[n], 16 * (NT // 4))

            state = ((c_sums, 0, F), (c_max, F, H), (c_denom, F + H, H))
            slot0 = ((c_he, 0, F), (c_score, F, H), (c_factor, F + H, H))
            with sp.If(sp.value_load(crowded_i[0:1, 0:1], min_val=0, max_val=NT) > 0):
                sp.wait_ge(c_ready, 2)
                for part, at, width in state:
                    sp.dma_start(carry_dram[:, at:at + width], part[FRESH:P, :]).then_inc(c_carried, 16)
                with sp.Fori(0, CHUNKS) as c:
                    sp.wait_ge(c_carried, (c + 1) * 48)
                    chunk = edges[0, bass.ds(c * (2 * FRESH), 2 * P)]
                    behind = edges[0, bass.ds(c * (2 * FRESH) + 2, 2 * P)]
                    sp.dma_start(c_cols[:, 0:2], chunk.rearrange("(s two) -> s two", two=2)).then_inc(c_cols_in, 16)
                    sp.dma_start(c_cols[:, 2:4], behind.rearrange("(s two) -> s two", two=2)).then_inc(c_cols_in, 16)
                    sp.dma_start(c_pairs, chunk.unsqueeze(0).broadcast_to([P, 2 * P])).then_inc(c_cols_in, 16)
                    sp.wait_ge(c_step, c * STEPS + 13)
                    for part, at, width in slot0:
                        sp.dma_start(part[0:1, :], carry_dram[:, at:at + width]).then_inc(c_state_in, 16)
                    sp.wait_ge(c_rows_out, (c + 1) * 16)
                    for part, at, width in state:
                        sp.dma_start(carry_dram[:, at:at + width], part[FRESH:P, :]).then_inc(c_carried, 16)
                sp.wait_ge(c_carried, (CHUNKS + 1) * 48)

        @block.gpsimd
        def _(pool):
            nc.gpsimd.iota(base_i[:, :], pattern=[[TR * P, TG]], base=0, channel_multiplier=P)
            nc.gpsimd.iota(brow_i[:, :], pattern=[[P, NT]], base=0, channel_multiplier=0)
            nc.gpsimd.iota(iota_i[:, :], pattern=[[1, P]], base=0, channel_multiplier=0)
            nc.gpsimd.memset(neg_half[:, :, :], -0.5)
            nc.gpsimd.memset(ident[:, :], 0.0).then_inc(pool_c, 1)
            pool.wait_ge(pool_c, 1)
            nc.gpsimd.affine_select(out=ident[:, :], in_=ident[:, :], compare_op=ALU.not_equal, fill=1.0, base=0,
                                    pattern=[[-1, P]], channel_multiplier=1).then_inc(pool_c, 1)
            pool.wait_ge(dve_c, 5)
            for g in range(TG):
                nc.gpsimd.indirect_dma_start(row_dst_i[:, g, :], None, edge_rows,
                                             bass.IndirectOffsetOnAxis(ap=row_i[:, g:g + 1], axis=0),
                                             bounds_check=ROWS - 1, oob_is_err=False).then_inc(rows_in, 16)
            pool.wait_ge(dve_c, 7)
            table = edges[:, 0:(E + PAD) // WIN * WIN * 2].rearrange("o (a b) -> (o a) b", b=2 * WIN)
            for g in range(TG):
                nc.gpsimd.indirect_dma_start(win_i[:, g, :], None, table,
                                             bass.IndirectOffsetOnAxis(ap=start_i[:, g:g + 1], axis=1)).then_inc(wins_in, 16)
            nc.gpsimd.memset(g_in[:, :, :], 0.0).then_inc(pool_c, 1)
            pool.wait_ge(*ready)

            def copy_idx(t):
                nc.gpsimd.tensor_copy(idx[:, t.ring(8):t.ring(8) + 4],
                                      idx_c[:, bass.ds(t.i * BODY + t.off, 4)]).then_inc(idx_cp, 1)

            def gather(t):
                nc.gpsimd.indirect_dma_start(g_in[:, t.ring(8), :], None, x,
                                             bass.IndirectOffsetOnAxis(ap=idx[:, t.ring(8):t.ring(8) + 1], axis=0),
                                             bounds_check=N - 1, oob_is_err=False).then_inc(g_ld[t.ring(8)], 16)

            def gather_may(t):
                pool.wait_ge(idx_cp, t.quads())
                wait(pool, he_done, t.count(back=8))
                if t.off % 4 == 3:
                    last = Tile(t.i, t.off - 4)
                    wait(pool, g_ld[last.ring(8)], last.turns(8) * 16)

            def invert_std(t):
                r = t.ring(4)
                pool.wait_ge(veps_done, t.turns(2))
                wait(pool, hn_done, t.count(back=4))
                wait(pool, he_done, t.count(back=4))
                nc.gpsimd.tensor_tensor(rstd[:, r - 1:r + 1, :], veps[:, r - 1:r + 1, :], neg_half[:, :, :],
                                        ALU.pow).then_inc(rstd_done, 1)

            def times_v1(t):
                pool.wait_ge(he_done, t.count())
                wait(pool, a1_done, t.count(back=2))
                nc.gpsimd.tensor_tensor(prod[:, t.ring(2), :], he[:, t.ring(8), :], v1[:, :],
                                        ALU.mult).then_inc(prod_done, 1)

            def weigh(t):
                pool.wait_ge(alpha_step, t.quads() * 3)
                pool.wait_ge(prod_done, t.count())
                rows = he[:, t.ring(8), :].rearrange("p (h d) -> p h d", h=H)
                by_head = alpha[:, t.off // QUAD % 2, t.off % QUAD, :].unsqueeze(2).broadcast_to([P, H, D])
                nc.gpsimd.tensor_tensor(rows, rows, by_head, ALU.mult).then_inc(scaled, 1)

            copy_idx(Tile(0, 0))
            copy_idx(Tile(0, 4))
            pool.wait_ge(idx_cp, 2)
            for k in range(G_LEAD):
                gather(Tile(0, k))
            invert_std(Tile(0, 1))
            pool.wait_ge(ld_v1, 32)

            def slots(i, ks):
                for k in ks:
                    ahead = Tile(i, k + G_LEAD)
                    if ahead.exists():
                        gather_may(ahead)
                    if Tile(i, k - AGG_LAG).exists():
                        weigh(Tile(i, k - AGG_LAG))
                    if Tile(i, k).exists():
                        times_v1(Tile(i, k))
                    if k % 2 and Tile(i, k + S_LEAD).exists():
                        invert_std(Tile(i, k + S_LEAD))
                    if ahead.exists():
                        gather(ahead)
                    if ahead.off % 4 == 3 and Tile(i, ahead.off + 1).exists():
                        copy_idx(Tile(i, ahead.off + 1))

            slots(0, range(BODY))
            with pool.Fori(1, WHOLE) as i:
                slots(i, range(BODY))
            slots(WHOLE, range(LEFT + AGG_LAG))

            with pool.If(pool.value_load(crowded_i[0:1, 0:1], min_val=0, max_val=NT) > 0):
                with pool.Fori(0, CHUNKS) as c:
                    pool.wait_ge(c_step, c * STEPS + 4)
                    nc.gpsimd.tensor_tensor(c_apart, c_row_dst, c_colf[:, 0:1].broadcast_to([P, P]),
                                            ALU.subtract).then_inc(c_apart_done, 1)
                    for into, col in ((c_src, 1), (c_dst, 0)):
                        nc.gpsimd.indirect_dma_start(into, None, x,
                                                     bass.IndirectOffsetOnAxis(ap=c_cols[:, col:col + 1], axis=0),
                                                     bounds_check=N - 1, oob_is_err=False).then_inc(c_rows_in, 16)
                    pool.wait_ge(c_step, c * STEPS + 7)
                    nc.gpsimd.tensor_tensor(c_rstd, c_veps, neg_half[:, 0, :], ALU.pow).then_inc(c_rstd_done, 1)
                    pool.wait_ge(c_step, c * STEPS + 24)
                    nc.gpsimd.tensor_tensor(c_idle, neg_half[:, 0, :], neg_half[:, 0, :], ALU.mult).then_inc(c_out_may, 1)
                    nc.gpsimd.indirect_dma_start(out, bass.IndirectOffsetOnAxis(ap=c_to_i, axis=0), c_out, None,
                                                 bounds_check=N - 1, oob_is_err=False).then_inc(c_rows_out, 16)

        @block.scalar
        def _(act):
            act.wait_ge(dve_c, 1)
            nc.scalar.activation(first_act[:, :], ones[:, :], ACT.Relu)

            def normalise(t):
                r, two = t.ring(4), t.ring(2)
                act.wait_ge(x_ld[t.ring(16)], t.turns(16) * 16)
                act.wait_ge(rstd_done, t.turns(2))
                act.wait_ge(shift_done, t.turns(2))
                wait(act, t_done, t.count(back=2) * 2)
                nc.scalar.activation(hn[:, two, :], x_in[:, t.ring(16), :], ACT.Relu, bias=shift[:, r, 0:1],
                                     scale=rstd[:, r, 0:1]).then_inc(hn_done, 1)

            def normalise_slots(t):
                r = t.ring(4)
                act.wait_ge(g_ld[t.ring(8)], t.turns(8) * 16)
                wait(act, g_mm, t.count(back=8) * 2)
                nc.scalar.activation(he[:, t.ring(8), :], g_in[:, t.ring(8), :], ACT.Relu, bias=shift[:, r, 1:2],
                                     scale=rstd[:, r, 1:2]).then_inc(he_done, 1)

            def keep_transposes(t):
                wait(act, out_mm, t.count(back=8) * 2)
                act.wait_ge(t_done, t.count() * 2 - 1)
                nc.scalar.copy(hT[:, t.ring(8), 0:HALF], tp[:, 0, 0:HALF]).then_inc(hT_done, 1)
                act.wait_ge(t_done, t.count() * 2)
                nc.scalar.copy(hT[:, t.ring(8), HALF:F + P], tp[:, 1, :]).then_inc(hT_done, 1)

            def keep_sums(t):
                wait(act, out_mm, t.count(back=2) * 2)
                for half in range(2):
                    act.wait_ge(g_mm, t.count() * 2 - 1 + half)
                    nc.scalar.copy(gT[:, t.ring(2), HALF * half:HALF * half + HALF],
                                   gp[:, half, 0:HALF]).then_inc(gT_done, 1)

            def slots(i, ks):
                for k in ks:
                    t, last, agg = Tile(i, k), Tile(i, k - 1), Tile(i, k - AGG_LAG)
                    soft_now = k % QUAD == 0 and last.exists()
                    if t.exists():
                        normalise(t)
                    if soft_now:
                        act.wait_ge(a2_tr, last.quads())
                        wait(act, z_mm, last.quads(back=1))
                        nc.scalar.copy(a2[:, :], a2_ps).then_inc(a2_sb, 1)
                    if t.exists():
                        normalise_slots(t)
                    if soft_now:
                        act.wait_ge(z_mm, last.quads())
                        wait(act, soft, last.quads(back=1) * SOFT)
                        nc.scalar.copy(z[:, :], z_ps).then_inc(z_sb, 1)
                    if t.exists():
                        keep_transposes(t)
                    if soft_now:
                        act.wait_ge(soft, last.quads(back=1) * SOFT + 4)
                        wait(act, alpha_tr, last.quads(back=1))
                        nc.scalar.activation(wt[:, :], m1[:, :], ACT.Exp).then_inc(exp_done, 1)
                    if agg.exists():
                        keep_sums(agg)

            slots(0, range(BODY))
            with act.Fori(1, WHOLE) as i:
                slots(i, range(BODY))
            slots(WHOLE, range(LEFT + AGG_LAG))

            with act.If(act.value_load(crowded_i[0:1, 0:1], min_val=0, max_val=NT) > 0):
                with act.Fori(0, CHUNKS) as c:
                    act.wait_ge(c_step, c * STEPS + 8)
                    for n, (into, rows_of) in enumerate(((c_he, c_src), (c_hd, c_dst))):
                        nc.scalar.activation(into, rows_of, ACT.Relu, bias=c_shift[:, n:n + 1],
                                             scale=c_rstd[:, n:n + 1]).then_inc(c_h_done, 1)
                    act.wait_ge(c_step, c * STEPS + 17)
                    nc.scalar.activation(c_weight, c_diff, ACT.Exp).then_inc(c_exp_done, 1)

        @block.vector
        def _(dve):
            v = nc.vector
            steps = [0]

            def step(ins):
                steps[0] += 1
                ins.then_inc(dve_c, 1)
                dve.wait_ge(dve_c, steps[0])

            def node_statistics(t):
                dve.wait_ge(x_ld[t.ring(16)], t.turns(16) * 16)
                for half in range(2):
                    last = v.bn_stats(stats[:, t.ring(4), half, :],
                                      x_in[:, t.ring(16), HALF * half:HALF * half + HALF])
                return last

            v.memset(w_bd[:, :], 0.0)
            v.memset(ones[:, :], 1.0)
            step(v.memset(wres_bd[:, :], 0.0))
            dve.wait_ge(pool_c, 1)
            v.tensor_copy(iota_row[:, :], iota_i[:, :])
            v.tensor_copy(base_c[:, :], base_i[:, :])
            step(v.tensor_copy(brow[:, :], brow_i[:, :]))
            v.tensor_scalar(brow_s[:, :], brow[:, :], float(FIRST_SHIFTED * P), float(-SHIFT), ALU.is_ge, ALU.mult)
            v.tensor_scalar(shift_c[:, :], base_c[:, :], float(FIRST_SHIFTED * P), float(-SHIFT), ALU.is_ge, ALU.mult)
            dve.wait_ge(ld_edges, 16)
            step(v.tensor_copy(row_first[:, :], rows_i[:, 0:1]))
            v.tensor_tensor(base_c[:, :], base_c[:, :], shift_c[:, :], ALU.add)
            v.tensor_tensor(brow[:, :], brow[:, :], brow_s[:, :], ALU.add).then_inc(bn_done, 1)
            dve.wait_ge(bn_done, 1)
            step(v.tensor_scalar(before[:, :], brow[:, :], row_first[:, 0:1], None, ALU.is_gt))
            dve.wait_ge(pe_c, 1)
            v.tensor_scalar(row_c[:, :], z_ps[0:TR, 0:TG], 1.0, 0.0, ALU.subtract, ALU.max).then_inc(bn_done, 1)
            dve.wait_ge(bn_done, 2)
            step(v.tensor_copy(row_i[:, :], row_c[:, :]))
            v.memset(v2[:, :, :], 0.0)
            v.memset(a1[:, :, :, :], 0.0)
            v.memset(seg[:, :, :, :], 0.0)
            v.memset(loc_c[:, :], -1.0)
            v.memset(idx_c[:, :], FAR)
            for k in range(EARLY // 2):
                node_statistics(Tile(0, k))
            dve.wait_ge(rows_in, 16 * TG)
            step(v.tensor_copy(row_dst[:, :, :], row_dst_i[:, :, :]))
            for g in range(TG):
                last = v.tensor_scalar(below[:, g, :], row_dst[:, g, :], base_c[:, g:g + 1], None, ALU.is_lt)
            last.then_inc(bn_done, 1)
            dve.wait_ge(bn_done, 3)
            v.tensor_reduce(below_n[:, :], below[:, :, :], AX.X, ALU.add).then_inc(bn_done, 1)
            dve.wait_ge(bn_done, 4)
            v.scalar_tensor_tensor(start_c[:, :], row_c[:, :], float(ROW), below_n[:, :], ALU.mult, ALU.add).then_inc(bn_done, 1)
            dve.wait_ge(bn_done, 5)
            step(v.tensor_scalar(start_i[:, :], start_c[:, :], 2.0, 2.0, ALU.mult, ALU.add))
            dve.wait_ge(pe_c, 2)
            for a in range(2):
                heads = v2[D * a:D * a + D, :, 0:H].rearrange("p q (r b) -> p q r b", b=2)
                for p in range(PAIRS):
                    v.tensor_copy(heads[:, p, p, a:a + 1], a2_ps[D * a:D * a + D, 2 * p + a:2 * p + a + 1])
            step(v.tensor_copy(v1_row[:, :], a2T_ps[0:H, 0:D]))
            for k in range(EARLY // 2, EARLY):
                node_statistics(Tile(0, k))
            dve.wait_ge(wins_in, 16 * TG)
            for g in range(TG):
                last = v.tensor_scalar(win_loc[:, g, :], win_pairs[:, g, :, 0], base_c[:, g:g + 1], None, ALU.subtract)
            last.then_inc(bn_done, 1)
            v.tensor_copy(win_src[:, :, :], win_pairs[:, :, 0:P, 1]).then_inc(bn_done, 1)
            dve.wait_ge(bn_done, 7)
            step(v.tensor_scalar(win_far[:, :, :], win_loc[:, :, 0:P], float(P), float(FAR), ALU.is_ge, ALU.mult))
            step(v.tensor_tensor(win_src[:, :, :], win_src[:, :, :], win_far[:, :, :], ALU.add))
            step(v.tensor_scalar(crowded[:, :], win_loc[:, :, P], float(P), None, ALU.is_lt))
            step(v.tensor_reduce(crowded_n[:, :], crowded[:, :], AX.X, ALU.add))
            step(v.tensor_tensor(seg[:, :, 1, 1:P], win_loc[:, :, 1:P], win_loc[:, :, 0:P - 1], ALU.is_equal))
            step(v.tensor_scalar(seg[:, :, 0, :], seg[:, :, 1, :], 1.0, -LOW, ALU.subtract, ALU.mult))
            for g in range(TG):
                dve.wait_ge(pe_c, 3 + g)
                v.tensor_copy(loc_c[:, TR * g:TR * g + TR], tp[:, g % 2, 0:TR])
                last = v.tensor_copy(idx_c[:, TR * g:TR * g + TR], tp[:, g % 2, P:P + TR])
                if g < 2:
                    step(last)
            dve.wait_ge(pe_c, 7)
            step(v.tensor_copy(crowded_i[:, :], z_ps[0:1, 0:1]))

            def copy_loc(t):
                wait(dve, oh_done, t.count(back=5))
                v.tensor_copy(loc[:, t.ring(8):t.ring(8) + 4],
                              loc_c[:, bass.ds(t.i * BODY + t.off, 4)]).then_inc(loc_cp, 1)

            def make_onehot(t):
                dve.wait_ge(loc_cp, t.quads())
                wait(dve, g_mm, t.count(back=16) * 2)
                wait(dve, t_done, t.count(back=16) * 2)
                v.tensor_scalar(onehot[:, t.ring(16), :], iota_row[:, :], loc[:, t.ring(8):t.ring(8) + 1], None,
                                ALU.is_equal).then_inc(oh_done, 1)

            def statistics(t):
                r = t.ring(4)
                if not (isinstance(t.i, int) and t.i * BODY + t.off < EARLY):
                    node_statistics(t)
                dve.wait_ge(g_ld[t.ring(8)], t.turns(8) * 16)
                for half in range(2):
                    last = v.bn_stats(stats[:, r, 2 + half, :], g_in[:, t.ring(8), HALF * half:HALF * half + HALF])
                last.then_inc(bn_done, 1)
                dve.wait_ge(bn_done, t.count() + 7)
                wait(dve, shift_done, t.turns(2, back=2))
                make_onehot(t)
                for kind in range(2):
                    last = v.bn_aggr(mv[:, r, kind, :], stats[:, r, 2 * kind:2 * kind + 2, :].rearrange("p a b -> p (a b)"))
                last.then_inc(mv_done, 1)

            def add_eps(t):
                r = t.ring(4)
                dve.wait_ge(mv_done, t.count())
                wait(dve, rstd_done, t.turns(2, back=2))
                v.tensor_scalar(veps[:, r - 1:r + 1, :], mv[:, r - 1:r + 1, :, 1], EPS, None, ALU.add).then_inc(veps_done, 1)

            def shifts(t):
                r = t.ring(4)
                dve.wait_ge(rstd_done, t.turns(2))
                wait(dve, he_done, t.count(back=4))
                wait(dve, hn_done, t.count(back=4))
                v.scalar_tensor_tensor(shift[:, r - 1:r + 1, :], mv[:, r - 1:r + 1, :, 0], -1.0, rstd[:, r - 1:r + 1, :],
                                       ALU.mult, ALU.mult).then_inc(shift_done, 1)

            def sum_heads(t):
                dve.wait_ge(prod_done, t.count())
                wait(dve, z_mm, t.quads(back=2))
                v.tensor_reduce(a1[:, t.off // QUAD % 2, t.off % QUAD, 0:H],
                                prod[:, t.ring(2), :].rearrange("p (h d) -> p h d", h=H), AX.X,
                                ALU.add).then_inc(a1_done, 1)

            def finish(t):
                wait(dve, o_st[t.ring(4)], t.turns(4, back=1) * 16)
                for half in range(2):
                    f = HALF * half
                    dve.wait_ge(out_mm, t.count() * 2 - 1 + half)
                    v.scalar_tensor_tensor(o[:, t.ring(4), f:f + HALF], op[:, half, 0:HALF], 0.0,
                                           x_in[:, t.ring(16), f:f + HALF], ALU.max, ALU.add).then_inc(o_done, 1)

            def keep_a2T(q):
                dve.wait_ge(a2T_mm, q.quads() * QUAD)
                wait(dve, a2_tr, q.quads(back=1))
                v.tensor_copy(a2T[:, :], a2T_ps).then_inc(a2T_sb, 1)

            def soft_step(q, n, ins):
                ins.then_inc(soft, 1)
                dve.wait_ge(soft, q.quads(back=1) * SOFT + n)

            def soft_max(q):
                par = q.off // QUAD % 2
                low = segq[:, par, 0, :]
                dve.wait_ge(z_sb, q.quads())
                soft_step(q, 1, v.scalar_tensor_tensor(score[:, :], z[:, :], SLOPE, z[:, :], ALU.mult, ALU.max))
                dve.wait_ge(seg_ld[par], q.turns(8) * 16)
                soft_step(q, 2, v.tensor_tensor_scan(m1[:, :], low[:, 0:P], score[:, :], LOW, ALU.add, ALU.max))
                soft_step(q, 3, v.tensor_tensor_scan(m2[:, ::-1], low[:, 1:WIN][:, ::-1], m1[:, ::-1], LOW,
                                                     ALU.add, ALU.max))
                soft_step(q, 4, v.tensor_tensor(m1[:, :], score[:, :], m2[:, :], ALU.subtract))

            def soft_sum(q):
                par = q.off // QUAD % 2
                same = segq[:, par, 1, :]
                dve.wait_ge(exp_done, q.quads())
                soft_step(q, 5, v.tensor_tensor_scan(s1[:, :], same[:, 0:P], wt[:, :], 0.0, ALU.mult, ALU.add))
                wait(dve, alpha_tr, q.quads(back=1))
                soft_step(q, 6, v.tensor_tensor_scan(s2[:, ::-1], same[:, 1:WIN][:, ::-1], s1[:, ::-1], 0.0,
                                                     ALU.mult, ALU.max))

            def alphas(q):
                par = q.off // QUAD % 2
                of_slot = lambda bank: bank.rearrange("p (a b) -> p a b", b=32)[:, :, 0:H]
                dve.wait_ge(alpha_tr, q.quads())
                v.tensor_scalar(denom[:, :, :], of_slot(s_ps), DENOM_MIN, None, ALU.max).then_inc(alpha_step, 1)
                dve.wait_ge(alpha_step, q.quads(back=1) * 3 + 1)
                v.reciprocal(rdenom[:, :, :], denom[:, :, :]).then_inc(alpha_step, 1)
                dve.wait_ge(alpha_step, q.quads(back=1) * 3 + 2)
                wait(dve, scaled, q.quads(back=2) * QUAD)
                v.tensor_tensor(alpha[:, par, :, :], of_slot(w_ps), rdenom[:, :, :], ALU.mult).then_inc(alpha_step, 1)

            copy_loc(Tile(0, 0))
            statistics(Tile(0, 0))
            statistics(Tile(0, 1))
            add_eps(Tile(0, 1))
            shifts(Tile(0, 1))

            def slots(i, ks):
                for k in ks:
                    t, nxt, q, late = Tile(i, k), Tile(i, k + S_LEAD), Tile(i, k - 1), Tile(i, k - OUT_LAG)
                    soft_now = k % QUAD == 0 and q.exists()
                    if soft_now:
                        keep_a2T(q)
                    if nxt.exists():
                        if nxt.off % 4 == 0:
                            copy_loc(nxt)
                        statistics(nxt)
                        if k % 2:
                            add_eps(nxt)
                    if late.exists():
                        finish(late)
                    if k % QUAD == 1 and Tile(i, k - 2).exists():
                        alphas(Tile(i, k - 2))
                    if soft_now:
                        soft_max(q)
                    if t.exists():
                        sum_heads(t)
                    if nxt.exists() and k % 2:
                        shifts(nxt)
                    if soft_now:
                        soft_sum(q)

            slots(0, range(BODY))
            with dve.Fori(1, WHOLE) as i:
                slots(i, range(BODY))
            slots(WHOLE, range(LEFT + OUT_LAG))

            with dve.If(dve.value_load(crowded_i[0:1, 0:1], min_val=0, max_val=NT) > 0):
                for n in range(4):
                    dve.wait_ge(o_st[n], 16 * (NT // 4))
                for part in (c_sums, c_max, c_denom, c_pick):
                    last = v.memset(part, 0.0)
                v.memset(c_factor, 1.0)
                last.then_inc(c_ready, 1)
                dve.wait_ge(c_ready, 1)
                v.tensor_copy(c_pick, ident[0:H, 0:H].unsqueeze(2).broadcast_to([H, H, P])).then_inc(c_ready, 1)
                with dve.Fori(0, CHUNKS) as c:
                    def step(n, ins):
                        ins.then_inc(c_step, 1)
                        dve.wait_ge(c_step, c * STEPS + n)

                    by_head = lambda a: a.rearrange("p (h d) -> p h d", h=H)
                    of_head = lambda a: a.unsqueeze(2).broadcast_to([P, H, D])
                    dve.wait_ge(c_cols_in, (c + 1) * 48)
                    v.tensor_copy(c_colf, c_cols)
                    step(1, v.tensor_copy(c_row_dst, c_pairs.rearrange("p (s two) -> p s two", two=2)[:, :, 0]))
                    step(2, v.tensor_tensor(c_more, c_colf[:, 0:1], c_colf[:, 2:3], ALU.is_equal))
                    step(3, v.scalar_tensor_tensor(c_to, c_more, float(FAR), c_colf[:, 0:1], ALU.mult, ALU.add))
                    step(4, v.tensor_copy(c_to_i, c_to))
                    dve.wait_ge(c_rows_in, (c + 1) * 32)
                    for n, rows_of in enumerate((c_src, c_dst)):
                        for half in range(2):
                            last = v.bn_stats(c_stats[:, 2 * n + half, :], rows_of[:, HALF * half:HALF * half + HALF])
                    step(5, last)
                    dve.wait_ge(c_apart_done, c + 1)
                    v.tensor_scalar(c_same, c_apart, 0.0, None, ALU.is_equal)
                    v.tensor_scalar(c_low, c_apart, 0.0, LOW, ALU.not_equal, ALU.mult)
                    for n in range(2):
                        last = v.bn_aggr(c_mv[:, n, :], c_stats[:, 2 * n:2 * n + 2, :].rearrange("p a b -> p (a b)"))
                    step(6, last)
                    step(7, v.tensor_scalar(c_veps, c_mv[:, :, 1], EPS, None, ALU.add))
                    dve.wait_ge(c_rstd_done, c + 1)
                    step(8, v.scalar_tensor_tensor(c_shift, c_mv[:, :, 0], -1.0, c_rstd, ALU.mult, ALU.mult))
                    dve.wait_ge(c_h_done, (c + 1) * 2)
                    step(9, v.tensor_tensor(c_prod, c_he, v1[:, :], ALU.mult))
                    step(10, v.tensor_reduce(c_a1, by_head(c_prod), AX.X, ALU.add))
                    dve.wait_ge(c_pe, c * 7 + 1)
                    for half in range(2):
                        last = v.tensor_copy(c_hdT[:, HALF * half:HALF * half + HALF], tp[:, half, 0:HALF])
                    step(11, last)
                    dve.wait_ge(c_pe, c * 7 + 2)
                    step(12, v.tensor_tensor(c_z, c_a1, c_a2_ps, ALU.add))
                    step(13, v.scalar_tensor_tensor(c_score, c_z, SLOPE, c_z, ALU.mult, ALU.max))
                    dve.wait_ge(c_pe, c * 7 + 3)
                    step(14, v.tensor_copy(c_scoreT, c_scoreT_ps))
                    dve.wait_ge(c_pe, c * 7 + 4)
                    for g, (bank, b) in enumerate(spread_at):
                        last = v.tensor_tensor(c_masked[:, 4 * g:4 * g + 4, :],
                                               bank[:, b, :].rearrange("p (h s) -> p h s", h=4),
                                               c_low.unsqueeze(1).broadcast_to([P, 4, P]), ALU.add)
                    step(15, last)
                    step(16, v.tensor_reduce(c_max, c_masked, AX.X, ALU.max))
                    step(17, v.tensor_tensor(c_diff, c_score, c_max, ALU.subtract))
                    dve.wait_ge(c_exp_done, c + 1)
                    v.tensor_tensor(c_dweight, c_weight, c_factor, ALU.mult)
                    step(18, v.tensor_tensor(by_head(c_prod), by_head(c_he), of_head(c_weight), ALU.mult))
                    dve.wait_ge(c_pe, c * 7 + 5)
                    for half in range(2):
                        v.tensor_copy(c_sums[:, HALF * half:HALF * half + HALF], gp[:, half, 0:HALF])
                    step(19, v.tensor_copy(c_denom, c_denom_ps))
                    step(20, v.tensor_scalar(c_dmin, c_denom, DENOM_MIN, None, ALU.max))
                    step(21, v.reciprocal(c_rden, c_dmin))
                    step(22, v.tensor_tensor(by_head(c_prod), by_head(c_sums), of_head(c_rden), ALU.mult))
                    dve.wait_ge(c_pe, c * 7 + 6)
                    for half in range(2):
                        last = v.tensor_copy(c_gT[:, HALF * half:HALF * half + HALF], tp[:, half, 0:HALF])
                    step(23, last)
                    dve.wait_ge(c_pe, c * 7 + 7)
                    for half in range(2):
                        f = HALF * half
                        last = v.scalar_tensor_tensor(c_out[:, f:f + HALF], op[:, half, 0:HALF], 0.0,
                                                      c_dst[:, f:f + HALF], ALU.max, ALU.add)
                    step(24, last)

        @block.tensor
        def _(pe):
            mm = nc.tensor.matmul
            pe.wait_ge(dve_c, 4)
            for g in range(TG):
                last = mm(z_ps[0:TR, g:g + 1], before[:, TR * g:TR * g + TR], ones[:, :], start=True, stop=True)
            last.then_inc(pe_c, 1)
            pe.wait_ge(ld_w, 16 * 8)
            pe.wait_ge(dve_c, 5)
            mm(a2T_ps[0:H, 0:D], al_t[:, :], w_twice[:, 0, :], start=True, stop=True)
            mm(a2_ps[:, 0:H], w_twice[:, :, :].rearrange("p a b -> p (a b)"), ar_t[:, :], start=True,
               stop=True).then_inc(pe_c, 1)
            pe.wait_ge(pool_c, 2)
            pe.wait_ge(dve_c, 10)
            for g in range(TG):
                if g >= 2:
                    pe.wait_ge(dve_c, 13 + g)
                nc.tensor.transpose(tp[:, g % 2, 0:TR], win_loc[:, g, 0:P], ident[0:TR, 0:TR])
                nc.tensor.transpose(tp[:, g % 2, P:P + TR], win_src[:, g, :], ident[0:TR, 0:TR]).then_inc(pe_c, 1)
            mm(z_ps[0:1, 0:1], crowded_n[:, :], ones[0:TR, :], start=True, stop=True).then_inc(pe_c, 1)
            pe.wait_ge(*ready)

            def transposes(t):
                r = t.ring(2)
                pe.wait_ge(hn_done, t.count())
                wait(pe, hT_done, t.count(back=1) * 2 - 1)
                for p in range(3):
                    last = nc.tensor.transpose(tp[:, 0, P * p:P * p + P], hn[:, r, P * p:P * p + P], ident[:, :])
                last.then_inc(t_done, 1)
                wait(pe, hT_done, t.count(back=1) * 2)
                for p in range(3):
                    nc.tensor.transpose(tp[:, 1, P * p:P * p + P], hn[:, r, P * (3 + p):P * (3 + p) + P], ident[:, :])
                pe.wait_ge(oh_done, t.count())
                nc.tensor.transpose(tp[:, 1, HALF:HALF + P], onehot[:, t.ring(16), :], ident[:, :]).then_inc(t_done, 1)

            def project_a2(t):
                j = t.off % QUAD
                pe.wait_ge(hT_done, t.count() * 2)
                if j == 0:
                    wait(pe, a2T_sb, t.quads(back=1))
                for p in range(PAIRS):
                    last = mm(a2T_ps[32 * j:32 * j + 32, :], v2[:, p, :], hT[:, t.ring(8), P * p:P * p + P],
                              start=(p == 0), stop=(p == PAIRS - 1))
                last.then_inc(a2T_mm, 1)

            def aggregate(t):
                pe.wait_ge(scaled, t.count())
                for half in range(2):
                    wait(pe, gT_done, t.count(back=1) * 2 - 1 + half)
                    for p in range(3):
                        f = P * (3 * half + p)
                        last = mm(gp[:, half, P * p:P * p + P], he[:, t.ring(8), f:f + P], onehot[:, t.ring(16), :],
                                  start=True, stop=True)
                    last.then_inc(g_mm, 1)

            def output(t, half):
                wait(pe, o_done, t.count(back=1) * 2 - 1 + half)
                pe.wait_ge(gT_done, t.count() * 2 - 1 + half)
                for p in range(3):
                    f = HALF * half + P * p
                    into = op[:, half, P * p:P * p + P]
                    mm(into, hT[:, t.ring(8), f:f + P], wres_bd[:, :], start=True, stop=False)
                    last = mm(into, gT[:, t.ring(2), f:f + P], w_bd[:, :], start=False, stop=True)
                last.then_inc(out_mm, 1)

            def turn_a2(q):
                pe.wait_ge(a2T_sb, q.quads())
                wait(pe, alpha_step, q.quads(back=1) * 3)
                nc.tensor.transpose(a2_ps, a2T[:, :], ident[:, :]).then_inc(a2_tr, 1)

            def sum_scores(q):
                pe.wait_ge(a2_sb, q.quads())
                pe.wait_ge(a1_done, q.quads() * QUAD)
                wait(pe, z_sb, q.quads(back=1))
                mm(z_ps, a1[:, q.off // QUAD % 2, :, :].rearrange("p a b -> p (a b)"), ident[:, :], start=True, stop=False)
                for j in range(QUAD):
                    slot = (q.off // QUAD * QUAD + j) % 8
                    last = mm(z_ps[32 * j:32 * j + 32, :], a2[:, 32 * j:32 * j + 32], hT[:, slot, F:F + P], start=False,
                              stop=True)
                last.then_inc(z_mm, 1)

            def turn_alpha(q):
                pe.wait_ge(soft, q.quads() * SOFT)
                nc.tensor.transpose(w_ps, wt[:, :], ident[:, :])
                nc.tensor.transpose(s_ps, s2[:, :], ident[:, :]).then_inc(alpha_tr, 1)

            def slots(i, ks):
                for k in ks:
                    t, q, agg, late = Tile(i, k), Tile(i, k - 1), Tile(i, k - AGG_LAG), Tile(i, k - OUT_LAG)
                    soft_now = k % QUAD == 0 and q.exists()
                    if k % QUAD == 1 and Tile(i, k - 2).exists():
                        if late.exists():
                            output(late, 0)
                        turn_alpha(Tile(i, k - 2))
                        if late.exists():
                            output(late, 1)
                    elif late.exists():
                        output(late, 0)
                        if soft_now:
                            turn_a2(q)
                        output(late, 1)
                    elif soft_now:
                        turn_a2(q)
                    if soft_now:
                        sum_scores(q)
                    if t.exists():
                        transposes(t)
                    if agg.exists():
                        aggregate(agg)
                    if t.exists():
                        project_a2(t)

            slots(0, range(BODY))
            with pe.Fori(1, WHOLE) as i:
                slots(i, range(BODY))
            slots(WHOLE, range(LEFT + OUT_LAG))

            with pe.If(pe.value_load(crowded_i[0:1, 0:1], min_val=0, max_val=NT) > 0):
                with pe.Fori(0, CHUNKS) as c:
                    def turn(rows_of):
                        for p in range(PAIRS):
                            last = nc.tensor.transpose(tp[:, p // 3, P * (p % 3):P * (p % 3) + P],
                                                       rows_of[:, P * p:P * p + P], ident[:, :])
                        last.then_inc(c_pe, 1)

                    pe.wait_ge(c_h_done, (c + 1) * 2)
                    turn(c_hd)
                    pe.wait_ge(c_step, c * STEPS + 11)
                    for p in range(PAIRS):
                        last = mm(c_a2_ps, c_hdT[:, P * p:P * p + P], v2[:, p, 0:H], start=(p == 0), stop=(p == PAIRS - 1))
                    last.then_inc(c_pe, 1)
                    pe.wait_ge(c_step, c * STEPS + 13)
                    pe.wait_ge(c_state_in, (c + 1) * 48)
                    nc.tensor.transpose(c_scoreT_ps, c_score, ident[:, :]).then_inc(c_pe, 1)
                    pe.wait_ge(c_step, c * STEPS + 14)
                    for h in range(H):
                        bank, b = spread_at[h // 4]
                        last = mm(bank[:, b, P * (h % 4):P * (h % 4) + P], c_pick[:, h, :], c_scoreT, start=True, stop=True)
                    last.then_inc(c_pe, 1)
                    pe.wait_ge(c_step, c * STEPS + 18)
                    for half in range(2):
                        mm(gp[:, half, 0:HALF], c_same, c_prod[:, HALF * half:HALF * half + HALF], start=True, stop=True)
                    mm(c_denom_ps, c_same, c_dweight, start=True, stop=True).then_inc(c_pe, 1)
                    pe.wait_ge(c_step, c * STEPS + 22)
                    turn(c_prod)
                    pe.wait_ge(c_step, c * STEPS + 23)
                    for p in range(PAIRS):
                        into = op[:, p // 3, P * (p % 3):P * (p % 3) + P]
                        mm(into, c_hdT[:, P * p:P * p + P], wres_bd[:, :], start=True, stop=False)
                        last = mm(into, c_gT[:, P * p:P * p + P], w_bd[:, :], start=False, stop=True)
                    last.then_inc(c_pe, 1)


def kernel(**inputs):
    import numpy as _np
    import concourse.bacc as _bacc
    from concourse import mybir as _mybir
    from concourse.bass_utils import run_bass_kernel_spmd as _run

    nc = _bacc.Bacc("TRN2", target_bir_lowering=False, num_devices=1)
    w, w_res = _np.asarray(inputs["L0_gnn_W"]), _np.asarray(inputs["L0_gnn_W_res"])
    edges = _np.full((1, E + PAD, 2), FAR, _np.int32)
    edges[0, 1:E + 1, 0], edges[0, 1:E + 1, 1] = inputs["dst"], inputs["src"]
    edges = edges.reshape(1, -1)
    laid_out = {
        "x": inputs["x"], "edges": edges, "dst": inputs["dst"],
        "w_t": w.T, "w": w, "w_res_t": w_res.T,
        "attn_l_t": _np.asarray(inputs["L0_gnn_attn_l"])[0].T,
        "attn_r_t": _np.asarray(inputs["L0_gnn_attn_r"])[0].T,
    }
    arrays, args = {}, []
    for name, a in laid_out.items():
        a = _np.ascontiguousarray(a)
        arrays[f"in_{name}"] = a
        args.append(nc.dram_tensor(f"in_{name}", a.shape, _mybir.dt.from_np(a.dtype), kind="ExternalInput").ap())
    out = nc.dram_tensor("out_0", (N, F), FP32, kind="ExternalOutput").ap()
    gnn(nc, *args, out)
    r = _run(nc, [arrays], core_ids=[0])
    return r.results[0]["out_0"]
```
